# Optimizing a Trainium2 kernel written in Bass

```python
import numpy as np
import jax
import jax.numpy as jnp

def _softmax(x, axis=-1):
    return jax.nn.softmax(x, axis=axis)

def _gelu(x):
    return jax.nn.gelu(x, approximate=True)

def _silu(x):
    return jax.nn.silu(x)

def _sigmoid(x):
    return jax.nn.sigmoid(x)

def _layernorm(x, axis=-1, eps=1e-05):
    m = jnp.mean(x, axis=axis, keepdims=True)
    v = jnp.var(x, axis=axis, keepdims=True)
    return (x - m) / jnp.sqrt(v + eps)

def _scatter_add(tgt, idx, src, axis=0):
    return tgt.at[idx].add(src)

def _segment_sum(src, seg, n):
    return jax.ops.segment_sum(src, seg, n)
kernel_name = 'mk_dlrm_tower_d1_rec_r8_35d7d6'

def setup_inputs(seed: int=0):
    np.random.seed(seed)
    _w = jnp.asarray

    def _rec_inputs():
        import jax
        import jax.numpy as jnp
        _tk = jax.random.key(seed)
        ids = jnp.stack([jax.random.randint(jax.random.fold_in(_tk, 200 + f), (512,), 0, v, jnp.int32) for f, v in enumerate([1000, 1000, 1000, 1000, 125000, 1250, 12500, 12500, 1250, 1250, 1000, 125000, 12500, 1000, 1250, 1250, 1250, 125000, 12500, 1000, 1250, 1250, 12500, 1000, 12500, 12500])], axis=1)
        tbl_0 = 0.05 * jax.random.normal(jax.random.fold_in(_tk, 500 + 0), (1000, 64), jnp.float32)
        tbl_1 = 0.05 * jax.random.normal(jax.random.fold_in(_tk, 500 + 1), (1000, 64), jnp.float32)
        tbl_2 = 0.05 * jax.random.normal(jax.random.fold_in(_tk, 500 + 2), (1000, 64), jnp.float32)
        tbl_3 = 0.05 * jax.random.normal(jax.random.fold_in(_tk, 500 + 3), (1000, 64), jnp.float32)
        tbl_4 = 0.05 * jax.random.normal(jax.random.fold_in(_tk, 500 + 4), (125000, 64), jnp.float32)
        tbl_5 = 0.05 * jax.random.normal(jax.random.fold_in(_tk, 500 + 5), (1250, 64), jnp.float32)
        tbl_6 = 0.05 * jax.random.normal(jax.random.fold_in(_tk, 500 + 6), (12500, 64), jnp.float32)
        tbl_7 = 0.05 * jax.random.normal(jax.random.fold_in(_tk, 500 + 7), (12500, 64), jnp.float32)
        tbl_8 = 0.05 * jax.random.normal(jax.random.fold_in(_tk, 500 + 8), (1250, 64), jnp.float32)
        tbl_9 = 0.05 * jax.random.normal(jax.random.fold_in(_tk, 500 + 9), (1250, 64), jnp.float32)
        tbl_10 = 0.05 * jax.random.normal(jax.random.fold_in(_tk, 500 + 10), (1000, 64), jnp.float32)
        tbl_11 = 0.05 * jax.random.normal(jax.random.fold_in(_tk, 500 + 11), (125000, 64), jnp.float32)
        tbl_12 = 0.05 * jax.random.normal(jax.random.fold_in(_tk, 500 + 12), (12500, 64), jnp.float32)
        tbl_13 = 0.05 * jax.random.normal(jax.random.fold_in(_tk, 500 + 13), (1000, 64), jnp.float32)
        tbl_14 = 0.05 * jax.random.normal(jax.random.fold_in(_tk, 500 + 14), (1250, 64), jnp.float32)
        tbl_15 = 0.05 * jax.random.normal(jax.random.fold_in(_tk, 500 + 15), (1250, 64), jnp.float32)
        tbl_16 = 0.05 * jax.random.normal(jax.random.fold_in(_tk, 500 + 16), (1250, 64), jnp.float32)
        tbl_17 = 0.05 * jax.random.normal(jax.random.fold_in(_tk, 500 + 17), (125000, 64), jnp.float32)
        tbl_18 = 0.05 * jax.random.normal(jax.random.fold_in(_tk, 500 + 18), (12500, 64), jnp.float32)
        tbl_19 = 0.05 * jax.random.normal(jax.random.fold_in(_tk, 500 + 19), (1000, 64), jnp.float32)
        tbl_20 = 0.05 * jax.random.normal(jax.random.fold_in(_tk, 500 + 20), (1250, 64), jnp.float32)
        tbl_21 = 0.05 * jax.random.normal(jax.random.fold_in(_tk, 500 + 21), (1250, 64), jnp.float32)
        tbl_22 = 0.05 * jax.random.normal(jax.random.fold_in(_tk, 500 + 22), (12500, 64), jnp.float32)
        tbl_23 = 0.05 * jax.random.normal(jax.random.fold_in(_tk, 500 + 23), (1000, 64), jnp.float32)
        tbl_24 = 0.05 * jax.random.normal(jax.random.fold_in(_tk, 500 + 24), (12500, 64), jnp.float32)
        tbl_25 = 0.05 * jax.random.normal(jax.random.fold_in(_tk, 500 + 25), (12500, 64), jnp.float32)
        _rk = jax.random.fold_in(_tk, 7)
        r_dense_t = 7.22013e-05 + 1.00017 * jax.random.normal(jax.random.fold_in(_rk, 101), (512, 256), jnp.float32)
        W_top1 = 0.0360844 * jax.random.normal(jax.random.fold_in(_tk, 801), (768, 512), jnp.float32)
        W_top2 = 0.0441942 * jax.random.normal(jax.random.fold_in(_tk, 802), (512, 256), jnp.float32)
        W_top3 = 0.0625 * jax.random.normal(jax.random.fold_in(_tk, 803), (256, 1), jnp.float32)
        b_top1 = jnp.zeros((512,), jnp.float32)
        b_top2 = jnp.zeros((256,), jnp.float32)
        return (r_dense_t, ids, tbl_0, tbl_1, tbl_2, tbl_3, tbl_4, tbl_5, tbl_6, tbl_7, tbl_8, tbl_9, tbl_10, tbl_11, tbl_12, tbl_13, tbl_14, tbl_15, tbl_16, tbl_17, tbl_18, tbl_19, tbl_20, tbl_21, tbl_22, tbl_23, tbl_24, tbl_25, W_top1, b_top1, W_top2, b_top2, W_top3)
    r_dense_t, ids, tbl_0, tbl_1, tbl_2, tbl_3, tbl_4, tbl_5, tbl_6, tbl_7, tbl_8, tbl_9, tbl_10, tbl_11, tbl_12, tbl_13, tbl_14, tbl_15, tbl_16, tbl_17, tbl_18, tbl_19, tbl_20, tbl_21, tbl_22, tbl_23, tbl_24, tbl_25, W_top1, b_top1, W_top2, b_top2, W_top3 = _rec_inputs()

    def _L0_rec_setup():
        import jax, jax.numpy as jnp
        import numpy as np
        EPS = 1e-05
        NI = 33
        TRIL_I, TRIL_J = np.tril_indices(NI, k=-1)

        def layer_norm(x, g, b):
            m = jnp.mean(x, axis=-1, keepdims=True)
            v = jnp.mean(jnp.square(x - m), axis=-1, keepdims=True)
            return (x - m) * jax.lax.rsqrt(v + EPS) * g + b
        key = jax.random.key(seed)
        ks = jax.random.split(key, 8)
        B, D_DENSE, N_SP, D_SP = (4096, 256, 26, 64)
        E, PROJ, MAXD, NFLAT = (128, 32, 512, 528)
        dense_t = jax.random.normal(ks[0], (B, D_DENSE), dtype=jnp.float32)
        sparse_t = jax.random.normal(ks[1], (B, N_SP, D_SP), dtype=jnp.float32)
        Wd = jax.random.normal(ks[2], (E, D_DENSE), dtype=jnp.float32) / np.sqrt(D_DENSE)
        Ws = jax.random.normal(ks[3], (E, D_SP), dtype=jnp.float32) / np.sqrt(D_SP)
        Wsi = jax.random.normal(ks[4], (PROJ, N_SP), dtype=jnp.float32) / np.sqrt(N_SP)
        Wl = jax.random.normal(ks[5], (MAXD, NFLAT), dtype=jnp.float32) / np.sqrt(NFLAT)
        gd = jnp.ones((E,), jnp.float32)
        bd = jnp.zeros((E,), jnp.float32)
        gs = jnp.ones((E,), jnp.float32)
        bs = jnp.zeros((E,), jnp.float32)
        gsi = jnp.ones((PROJ,), jnp.float32)
        bsi = jnp.zeros((PROJ,), jnp.float32)
        gl = jnp.ones((MAXD,), jnp.float32)
        bl = jnp.zeros((MAXD,), jnp.float32)
        return {'dense_t': dense_t, 'sparse_t': sparse_t, 'Wd': Wd, 'gd': gd, 'bd': bd, 'Ws': Ws, 'gs': gs, 'bs': bs, 'Wsi': Wsi, 'gsi': gsi, 'bsi': bsi, 'Wl': Wl, 'gl': gl, 'bl': bl, 'dims_in_use': 384}
    _L0_rec_all = _L0_rec_setup()
    _L0_rec_in = {k: v for k, v in _L0_rec_all.items() if k in ('Wd', 'gd', 'bd', 'Ws', 'gs', 'bs', 'Wsi', 'gsi', 'bsi', 'Wl', 'gl', 'bl')}
    del _L0_rec_all
    return {'r_dense_t': r_dense_t, 'ids': ids, 'tbl_0': tbl_0, 'tbl_1': tbl_1, 'tbl_2': tbl_2, 'tbl_3': tbl_3, 'tbl_4': tbl_4, 'tbl_5': tbl_5, 'tbl_6': tbl_6, 'tbl_7': tbl_7, 'tbl_8': tbl_8, 'tbl_9': tbl_9, 'tbl_10': tbl_10, 'tbl_11': tbl_11, 'tbl_12': tbl_12, 'tbl_13': tbl_13, 'tbl_14': tbl_14, 'tbl_15': tbl_15, 'tbl_16': tbl_16, 'tbl_17': tbl_17, 'tbl_18': tbl_18, 'tbl_19': tbl_19, 'tbl_20': tbl_20, 'tbl_21': tbl_21, 'tbl_22': tbl_22, 'tbl_23': tbl_23, 'tbl_24': tbl_24, 'tbl_25': tbl_25, 'W_top1': W_top1, 'b_top1': b_top1, 'W_top2': W_top2, 'b_top2': b_top2, 'W_top3': W_top3, 'L0_rec_Wd': _L0_rec_in['Wd'], 'L0_rec_gd': _L0_rec_in['gd'], 'L0_rec_bd': _L0_rec_in['bd'], 'L0_rec_Ws': _L0_rec_in['Ws'], 'L0_rec_gs': _L0_rec_in['gs'], 'L0_rec_bs': _L0_rec_in['bs'], 'L0_rec_Wsi': _L0_rec_in['Wsi'], 'L0_rec_gsi': _L0_rec_in['gsi'], 'L0_rec_bsi': _L0_rec_in['bsi'], 'L0_rec_Wl': _L0_rec_in['Wl'], 'L0_rec_gl': _L0_rec_in['gl'], 'L0_rec_bl': _L0_rec_in['bl']}

def reference(r_dense_t, ids, tbl_0, tbl_1, tbl_2, tbl_3, tbl_4, tbl_5, tbl_6, tbl_7, tbl_8, tbl_9, tbl_10, tbl_11, tbl_12, tbl_13, tbl_14, tbl_15, tbl_16, tbl_17, tbl_18, tbl_19, tbl_20, tbl_21, tbl_22, tbl_23, tbl_24, tbl_25, W_top1, b_top1, W_top2, b_top2, W_top3, L0_rec_Wd, L0_rec_gd, L0_rec_bd, L0_rec_Ws, L0_rec_gs, L0_rec_bs, L0_rec_Wsi, L0_rec_gsi, L0_rec_bsi, L0_rec_Wl, L0_rec_gl, L0_rec_bl):
    import jax
    import jax.numpy as jnp

    def _L0_rec_ref(dense_t, sparse_t, Wd, gd, bd, Ws, gs, bs, Wsi, gsi, bsi, Wl, gl, bl, dims_in_use):
        import jax, jax.numpy as jnp
        import numpy as np
        EPS = 1e-05
        NI = 33
        TRIL_I, TRIL_J = np.tril_indices(NI, k=-1)

        def layer_norm(x, g, b):
            m = jnp.mean(x, axis=-1, keepdims=True)
            v = jnp.mean(jnp.square(x - m), axis=-1, keepdims=True)
            return (x - m) * jax.lax.rsqrt(v + EPS) * g + b
        x = layer_norm(dense_t @ Wd.T, gd, bd)
        y = layer_norm(jnp.einsum('bnd,ed->bne', sparse_t, Ws), gs, bs)
        y = jnp.einsum('bne,pn->bep', y, Wsi)
        y = layer_norm(y, gsi, bsi)
        y = jnp.swapaxes(y, 1, 2)
        T = jnp.concatenate([x[:, None, :], y], axis=1)
        Z = jnp.einsum('bnd,bmd->bnm', T, T)
        Zflat = Z[:, TRIL_I, TRIL_J]
        out = layer_norm(Zflat @ Wl.T, gl, bl)
        maxd = out.shape[-1]
        mask = (jnp.arange(maxd) < dims_in_use).astype(out.dtype)
        return out * mask
    e = jnp.stack([tbl_0[ids[:, 0]], tbl_1[ids[:, 1]], tbl_2[ids[:, 2]], tbl_3[ids[:, 3]], tbl_4[ids[:, 4]], tbl_5[ids[:, 5]], tbl_6[ids[:, 6]], tbl_7[ids[:, 7]], tbl_8[ids[:, 8]], tbl_9[ids[:, 9]], tbl_10[ids[:, 10]], tbl_11[ids[:, 11]], tbl_12[ids[:, 12]], tbl_13[ids[:, 13]], tbl_14[ids[:, 14]], tbl_15[ids[:, 15]], tbl_16[ids[:, 16]], tbl_17[ids[:, 17]], tbl_18[ids[:, 18]], tbl_19[ids[:, 19]], tbl_20[ids[:, 20]], tbl_21[ids[:, 21]], tbl_22[ids[:, 22]], tbl_23[ids[:, 23]], tbl_24[ids[:, 24]], tbl_25[ids[:, 25]]], axis=1)
    z = _L0_rec_ref(r_dense_t, e, L0_rec_Wd, L0_rec_gd, L0_rec_bd, L0_rec_Ws, L0_rec_gs, L0_rec_bs, L0_rec_Wsi, L0_rec_gsi, L0_rec_bsi, L0_rec_Wl, L0_rec_gl, L0_rec_bl, 384)
    z = z.reshape(z.shape[0], -1)
    h = jnp.concatenate([z, r_dense_t], axis=1)
    h = jnp.maximum(h @ W_top1 + b_top1, 0.0)
    h = jnp.maximum(h @ W_top2 + b_top2, 0.0)
    y = h @ W_top3
    return y

_drawn_inputs = setup_inputs


def setup_inputs(seed=0):
    import zlib

    import numpy as np

    out = dict(_drawn_inputs(seed))
    spreads = {'b_top1': (0.0, 0.1),
     'b_top2': (0.0, 0.1),
     'L0_rec_gd': (1.0, 0.6),
     'L0_rec_bd': (0.0, 0.8),
     'L0_rec_gs': (1.0, 0.6),
     'L0_rec_bs': (0.0, 0.1),
     'L0_rec_gsi': (1.0, 0.2),
     'L0_rec_bsi': (0.0, 0.1),
     'L0_rec_gl': (1.0, 0.2),
     'L0_rec_bl': (0.0, 0.1)}
    factors = {}
    for name, (base, spread) in spreads.items():
        noise = np.random.default_rng([zlib.crc32(name.encode()), seed]).standard_normal(out[name].shape)
        drawn = base * np.exp(spread * noise) if base else spread * noise
        out[name] = jnp.asarray(drawn.astype(out[name].dtype))
    for name, factor in factors.items():
        out[name] = (out[name] * factor).astype(out[name].dtype)
    return out
```

```python
from contextlib import ExitStack

import concourse.bass as bass
import numpy as np
from concourse import mybir

P = 128
BATCH, N_SPARSE, D_SPARSE, D_DENSE = 512, 26, 64, 256
E, PROJ, MAXD, DIMS_IN_USE = 128, 32, 512, 384
H1, H2 = 512, 256
EPS = 1e-5

QUARTERS = 4
QB = BATCH // QUARTERS
UNITS = 8
UB = QB // UNITS
TILES = QB * N_SPARSE // P
PERIOD = TILES // 2
BLOCK = 4
GROUPS = QB // BLOCK
CW = PROJ + 2
BT = BLOCK * PROJ
BW = BT + BLOCK + 1
HALVES = 2
HB = UB // BLOCK // HALVES
KD = D_DENSE // P
KZ = DIMS_IN_USE // P
KTOP = KZ + KD
K1, K2 = H1 // P, H2 // P
XROWS = 2 * PROJ + 2
PAIR_TILES = 6
HALFP = PROJ // 2


def chunk_pairs():
    need = [-(-(UB * N_SPARSE * (u + 1)) // (2 * P)) for u in range(UNITS)]
    return [(a, b) for a, b in zip([0] + need[:-1], need)]


def segments():
    out, col = [], 0
    for u in range(UNITS // 2):
        segs = []
        lo, hi = UB * u, UB * (u + 1)
        for t in range(PERIOD):
            first = max(lo, t * P // N_SPARSE)
            last = min(hi - 1, (t * P + P - 1) // N_SPARSE)
            if first <= last:
                segs.append((t, first - lo, last - first + 1, col))
                col += (last - first + 1) * PROJ
        out.append(segs)
    return out, col


CHUNKS = chunk_pairs()
MIX, MIX_COLS = segments()


def pair_rows():
    rows = []
    for kt in range(PAIR_TILES):
        for k in range(P):
            if kt < 4:
                rows.append((k % PROJ, 4 * kt + k // PROJ))
            else:
                rows.append((HALFP + k % HALFP, HALFP + 8 * (kt - 4) + k // HALFP))
    return rows


def tower(nc, tables, ids, bases, eye, ws, wmix, gs, bs, dense, wd, gd, bd, wl, wlx, gpq, bpq, fold, foldx, xscale,
          w1, b1, w2, b2, w3, gl, bl, out):
    f32, i32 = mybir.dt.float32, mybir.dt.int32
    ALU, ACT, AX = mybir.AluOpType, mybir.ActivationFunctionType, mybir.AxisListType

    scratch = nc.dram_tensor("pairs_scratch", (CW, PROJ, BLOCK, GROUPS), f32, kind="Internal").ap()

    ctx = ExitStack()
    with ctx:
        def sb(name, shape, dt=f32):
            return ctx.enter_context(nc.sbuf_tensor(name, shape, dt))

        def bank(name):
            return ctx.enter_context(nc.psum_tensor(name, [P, 512], f32))

        def sem(name):
            return ctx.enter_context(nc.semaphore(name))

        ids_sb = sb("ids_sb", [P, QUARTERS * TILES], i32)
        bases_sb = sb("bases_sb", [P, QUARTERS * TILES], i32)
        rows_sb = sb("rows_sb", [P, QUARTERS * TILES], i32)
        eye_sb = sb("eye_sb", [P, P])
        emb = sb("emb", [P, TILES, D_SPARSE])
        embT = sb("embT", [P, 2, 2 * P])
        ws_sb = sb("ws_sb", [P, 2, E])
        ws_mean = sb("ws_mean", [P, 2])
        sq1 = sb("sq1", [P, 2, 4, E])
        ss1 = sb("ss1", [P, 2, 4])
        std1 = sb("std1", [P, 2, 4])
        rstd1 = sb("rstd1", [P, 2, 4])
        yn = sb("yn", [P, TILES, E])
        mix_sb = sb("mix_sb", [P, MIX_COLS // PROJ, PROJ])
        mix_mean = sb("mix_mean", [P, MIX_COLS // PROJ])
        gs_sb = sb("gs_sb", [E, 1])
        bs_rep = sb("bs_rep", [N_SPARSE, E])
        shift = sb("shift", [E, PROJ])
        y2 = sb("y2", [E, 2, UB, PROJ])
        sq2 = sb("sq2", [E, 2, UB, PROJ])
        ss2 = sb("ss2", [E, 2, UB])
        std2 = sb("std2", [E, 2, UB])
        rstd2 = sb("rstd2", [E, 2, UB])
        tx = sb("tx", [E, 2, UB // BLOCK, BW])
        crossed = sb("crossed", [P, BW, GROUPS])
        pairsT = sb("pairsT", [P, PAIR_TILES, QB])
        extraT = sb("extraT", [P, QB])
        dense_sb = sb("dense_sb", [P, KD, BATCH])
        wd_sb = sb("wd_sb", [P, KD, E])
        gd_sb = sb("gd_sb", [E, 1])
        bd_sb = sb("bd_sb", [E, 1])
        xstat = sb("xstat", [P, QUARTERS, 6])
        xmv = sb("xmv", [P, QUARTERS, 2])
        xstd = sb("xstd", [P, QUARTERS])
        xrstd = sb("xrstd", [P, QUARTERS])
        xn = sb("xn", [P, QUARTERS, E])
        xT = sb("xT", [E, QUARTERS, BLOCK, GROUPS])
        sx = sb("sx", [1, BATCH])
        ones = sb("ones", [P, 1])
        eps = sb("eps", [P, 1])
        wl_sb = sb("wl_sb", [P, PAIR_TILES, MAXD])
        wlx_sb = sb("wlx_sb", [PROJ, MAXD])
        wx = sb("wx", [XROWS, MAXD])
        gpq_sb = sb("gpq_sb", [P, 2, PAIR_TILES])
        bpq_sb = sb("bpq_sb", [P, 2, PAIR_TILES])
        gg = sb("gg", [P, PAIR_TILES])
        fold_sb = sb("fold_sb", [P, PAIR_TILES, XROWS])
        foldx_sb = sb("foldx_sb", [PROJ, XROWS])
        xscale_sb = sb("xscale_sb", [XROWS, 1])
        w1_sb = sb("w1_sb", [P, KTOP, H1])
        b1_sb = sb("b1_sb", [P, K1])
        bias1 = sb("bias1", [P, K1])
        w2_sb = sb("w2_sb", [P, K1, H2])
        b2_sb = sb("b2_sb", [P, K2])
        w3_sb = sb("w3_sb", [P, K2])
        gl_sb = sb("gl_sb", [P, KZ])
        bl_sb = sb("bl_sb", [P, KZ])
        wstat = sb("wstat", [P, 6])
        wmv = sb("wmv", [P, 2])
        wstd = sb("wstd", [P, 1])
        wrstd = sb("wrstd", [P, 1])
        zn = sb("zn", [P, DIMS_IN_USE])
        hz = sb("hz", [P, KZ, QB])
        h1 = sb("h1", [P, K1, QB])
        h2 = sb("h2", [P, K2, QB])
        y_all = sb("y_all", [1, QUARTERS, QB])

        pT = bank("pT")
        pY = [bank("pY0"), bank("pY1")]
        pA = [bank("pA0"), bank("pA1")]
        pZ = [bank("pZ0"), bank("pZ1")]
        pW = bank("pW")

        ids_in = sem("ids_in")
        ws_in = sem("ws_in")
        dense_in = sem("dense_in")
        mix_in = sem("mix_in")
        wl_in = sem("wl_in")
        top_in = sem("top_in")
        rows_ready = sem("rows_ready")
        consts_ready = sem("consts_ready")
        ws_steps = sem("ws_steps")
        mix_steps = sem("mix_steps")
        x_projected = sem("x_projected")
        x_stats = sem("x_stats")
        x_std = sem("x_std")
        x_rstd = sem("x_rstd")
        x_normed = sem("x_normed")
        x_transposed = sem("x_transposed")
        x_ready = sem("x_ready")
        shift_made = sem("shift_made")
        shift_ready = sem("shift_ready")
        sx_made = sem("sx_made")
        sx_ready = sem("sx_ready")
        gg_ready = sem("gg_ready")
        fold_ready = sem("fold_ready")
        wx_made = sem("wx_made")
        wx_ready = sem("wx_ready")
        wl_ready = sem("wl_ready")
        bias1_made = sem("bias1_made")
        w1_ready = sem("w1_ready")
        gathered = [sem(f"gathered{u}") for u in range(UNITS)]
        transposed = sem("transposed")
        embT_ready = sem("embT_ready")
        projected = sem("projected")
        squared1 = sem("squared1")
        summed1 = sem("summed1")
        std1_ready = sem("std1_ready")
        rstd1_ready = sem("rstd1_ready")
        yn_ready = sem("yn_ready")
        mixed = sem("mixed")
        y2_ready = sem("y2_ready")
        squared2 = sem("squared2")
        summed2 = sem("summed2")
        std2_ready = sem("std2_ready")
        rstd2_ready = sem("rstd2_ready")
        x_placed = sem("x_placed")
        t_ready = sem("t_ready")
        cross_done = sem("cross_done")
        cross_copied = sem("cross_copied")
        pairs_out = sem("pairs_out")
        pairs_in = sem("pairs_in")
        linked = sem("linked")
        link_stats = sem("link_stats")
        link_mean = sem("link_mean")
        link_std = sem("link_std")
        link_rstd = sem("link_rstd")
        z_ready = sem("z_ready")
        z_transposed = sem("z_transposed")
        hz_ready = sem("hz_ready")
        top1_done = sem("top1_done")
        h1_ready = sem("h1_ready")
        top2_done = sem("top2_done")
        h2_ready = sem("h2_ready")
        top3_done = sem("top3_done")
        pW_free = sem("pW_free")
        y_out = sem("y_out")

        def after(eng, semaphore, value):
            if not (isinstance(value, int) and value <= 0):
                eng.wait_ge(semaphore, value)

        def quarters(eng, step, last_lag):
            for s in range(UNITS):
                step(0, s)
            with eng.Fori(1, QUARTERS) as i:
                for s in range(UNITS):
                    step(i, s)
            for s in range(last_lag + 1):
                step(QUARTERS, s)

        def unit(i, s, lag):
            q, u = (i, s - lag) if s >= lag else (i - 1, s - lag + UNITS)
            if isinstance(i, int) and (q < 0 or q >= QUARTERS):
                return None
            return q, u

        def quarter_step(i, s, at):
            return s == at and not (isinstance(i, int) and i == 0)

        LAG_Y, LAG_A, LAG_Z = 1, 2, 3
        SLOT_LINK, SLOT_TRANSPOSE, SLOT_TOP1, SLOT_TOP2, SLOT_TOP3 = 4, 5, 6, 7, 7

        block = ctx.enter_context(nc.Block())

        @block.gpsimd
        def _(pool):
            pool.wait_ge(rows_ready, 1)
            for q in range(QUARTERS):
                for u in range(UNITS):
                    lo, hi = 2 * CHUNKS[u][0], 2 * CHUNKS[u][1]
                    after(pool, transposed, UNITS * (q - 1) + u + 1)
                    for t in range(lo, hi):
                        c = q * TILES + t
                        nc.gpsimd.indirect_dma_start(
                            emb[:, t, :], None, tables[:, :],
                            bass.IndirectOffsetOnAxis(rows_sb[:, c:c + 1], 0)).then_inc(gathered[u], 16)

        @block.sync
        def _(sp):
            sp.dma_start(ids_sb[:, :], ids).then_inc(ids_in, 16)
            sp.dma_start(bases_sb[:, :], bases).then_inc(ids_in, 16)
            sp.dma_start(ws_sb[:, :, :], ws).then_inc(ws_in, 16)
            sp.dma_start(eye_sb[:, :], eye).then_inc(ws_in, 16)
            sp.dma_start(dense_sb[:, :, :], dense).then_inc(dense_in, 16)
            sp.dma_start(wd_sb[:, :, :], wd).then_inc(dense_in, 16)
            sp.dma_start(gd_sb[:, :], gd).then_inc(dense_in, 16)
            sp.dma_start(bd_sb[:, :], bd).then_inc(dense_in, 16)
            sp.dma_start(mix_sb[:, :, :], wmix).then_inc(mix_in, 16)
            sp.dma_start(gs_sb[:, :], gs).then_inc(mix_in, 16)
            sp.dma_start(bs_rep[:, :], bs.broadcast_to([N_SPARSE, E])).then_inc(mix_in, 16)
            sp.dma_start(wl_sb[:, :, :], wl).then_inc(wl_in, 16)
            sp.dma_start(wlx_sb[:, :], wlx).then_inc(wl_in, 16)
            sp.dma_start(gpq_sb[:, :, :], gpq).then_inc(wl_in, 16)
            sp.dma_start(bpq_sb[:, :, :], bpq).then_inc(wl_in, 16)
            sp.dma_start(fold_sb[:, :, :], fold).then_inc(wl_in, 16)
            sp.dma_start(foldx_sb[:, :], foldx).then_inc(wl_in, 16)
            sp.dma_start(xscale_sb[:, :], xscale).then_inc(wl_in, 16)
            sp.dma_start(w1_sb[:, :, :], w1).then_inc(top_in, 16)
            sp.dma_start(b1_sb[:, :], b1).then_inc(top_in, 16)
            sp.dma_start(w2_sb[:, :, :], w2).then_inc(top_in, 16)
            sp.dma_start(b2_sb[:, :], b2).then_inc(top_in, 16)
            sp.dma_start(w3_sb[:, :], w3).then_inc(top_in, 16)
            sp.dma_start(gl_sb[:, :], gl).then_inc(top_in, 16)
            sp.dma_start(bl_sb[:, :], bl).then_inc(top_in, 16)
            sp.wait_ge(sx_ready, 1)
            sp.wait_ge(consts_ready, 1)

            def store_pairs(q):
                sp.wait_ge(cross_copied, HALVES * UNITS * (q + 1))
                for b4 in range(BLOCK):
                    sp.dma_start(scratch[0:PROJ, :, b4, :].rearrange("c p g -> p c g"),
                                 crossed[PROJ * b4:PROJ * (b4 + 1), PROJ * b4:PROJ * (b4 + 1), :]
                                 ).then_inc(pairs_out, 16)
                    sp.dma_start(scratch[PROJ:CW, :, b4, :].rearrange("c p g -> p c g"),
                                 crossed[PROJ * b4:PROJ * (b4 + 1), BT + b4:BW:BLOCK - b4, :]).then_inc(pairs_out, 16)

            def load_pairs(q):
                sp.wait_ge(pairs_out, 32 * BLOCK * (q + 1))
                rows = scratch.rearrange("c p b g -> c p (b g)")
                sp.dma_start(pairsT[:, 0:4, :],
                             rows[0:HALFP].rearrange("(t c) p b -> (c p) t b", t=4)).then_inc(pairs_in, 16)
                for t in range(2):
                    c0 = HALFP + 8 * t
                    sp.dma_start(pairsT[:, 4 + t, :], rows[c0:c0 + 8, HALFP:PROJ, :]).then_inc(pairs_in, 16)
                sp.dma_start(extraT[0:2 * PROJ, :],
                             rows[PROJ:CW].rearrange("c p b -> (c p) b")).then_inc(pairs_in, 16)
                sp.wait_ge(sx_ready, 1)
                sp.dma_start(extraT[2 * PROJ:2 * PROJ + 1, :], sx[0:1, bass.ts(q, QB)]).then_inc(pairs_in, 16)

            store_pairs(0)
            load_pairs(0)
            with sp.Fori(1, QUARTERS) as q:
                sp.wait_ge(pairs_in, 80 * q)
                store_pairs(q)
                sp.wait_ge(sx_ready, 1)
                sp.wait_ge(linked, q)
                load_pairs(q)
            sp.wait_ge(pW_free, QUARTERS + 1)
            sp.dma_start(out, y_all[:, :, :]).then_inc(y_out, 16)
            sp.wait_ge(y_out, 16)

        @block.tensor
        def _(pe):
            def prepare():
                pe.wait_ge(dense_in, 64)
                for t in range(QUARTERS):
                    for k in range(KD):
                        mm = nc.tensor.matmul(pW[:, E * t:E * (t + 1)], dense_sb[:, k, P * t:P * (t + 1)],
                                              wd_sb[:, k, :], start=k == 0, stop=k == KD - 1)
                mm.then_inc(x_projected, 1)
                pe.wait_ge(x_normed, 1)
                pe.wait_ge(ws_in, 32)
                for t in range(QUARTERS):
                    mm = nc.tensor.transpose(pA[0][:, P * t:P * (t + 1)], xn[:, t, :], eye_sb[:, :])
                mm.then_inc(x_transposed, 1)

            def prepare_mix():
                pe.wait_ge(mix_steps, 3)
                nc.tensor.matmul(pW[:, 0:PROJ], bs_rep[:, :], mix_sb[0:N_SPARSE, 0, :],
                                 start=True, stop=True).then_inc(shift_made, 1)
                pe.wait_ge(shift_ready, 1)
                pe.wait_ge(x_ready, 1)
                nc.tensor.matmul(pW[0:1, :], ones[:, :], xT[:, :, :, :].rearrange("e q b g -> e (q b g)"),
                                 start=True, stop=True).then_inc(sx_made, 1)

            def prepare_link():
                pe.wait_ge(fold_ready, 1)
                pe.wait_ge(sx_ready, 1)
                for k in range(PAIR_TILES):
                    nc.tensor.matmul(pW[0:XROWS, :], fold_sb[:, k, :], wl_sb[:, k, :], start=k == 0, stop=False)
                nc.tensor.matmul(pW[0:XROWS, :], foldx_sb[:, :], wlx_sb[:, :],
                                 start=False, stop=True).then_inc(wx_made, 1)

            def prepare_top():
                pe.wait_ge(top_in, 112)
                pe.wait_ge(wx_ready, 1)
                for c in range(K1):
                    for k in range(KZ):
                        mm = nc.tensor.matmul(pW[:, c:c + 1], w1_sb[:, k, P * c:P * (c + 1)], bl_sb[:, k:k + 1],
                                              start=k == 0, stop=k == KZ - 1)
                mm.then_inc(bias1_made, 1)

            def stage_t(q, u):
                n = UNITS * q + u
                lo, hi = CHUNKS[u]
                pe.wait_ge(gathered[u], 32 * (hi - lo) * (q + 1))
                after(pe, embT_ready, n)
                for j in range(lo, hi):
                    mm = nc.tensor.transpose(pT[:, P * (j - lo):P * (j - lo + 1)],
                                             emb[:, 2 * j:2 * j + 2, :].rearrange("p t d -> p (t d)"), eye_sb[:, :])
                mm.then_inc(transposed, 1)

            def stage_y(q, u):
                n = UNITS * q + u
                lo, hi = CHUNKS[u]
                pe.wait_ge(embT_ready, n + 1)
                after(pe, yn_ready, n - 1)
                for j in range(hi - lo):
                    mm = nc.tensor.matmul(pY[u % 2][:, 2 * E * j:2 * E * (j + 1)], embT[:, u % 2, P * j:P * (j + 1)],
                                          ws_sb[:, :, :].rearrange("p t e -> p (t e)"), start=True, stop=True)
                mm.then_inc(projected, 1)

            def stage_a(q, u):
                n = UNITS * q + u
                pe.wait_ge(yn_ready, n + 1)
                after(pe, y2_ready, n - 1)
                segs = MIX[u % len(MIX)]
                for t, first, count, col in segs:
                    tile = PERIOD * (u // len(MIX)) + t
                    mm = nc.tensor.matmul(
                        pA[u % 2][:, PROJ * first:PROJ * (first + count)], yn[:, tile, :],
                        mix_sb[:, col // PROJ:col // PROJ + count, :].rearrange("p b c -> p (b c)"),
                        start=t == segs[0][0], stop=t == segs[-1][0], skip_group_check=True)
                mm.then_inc(mixed, 1)

            def stage_z(q, u):
                n = UNITS * q + u
                pe.wait_ge(t_ready, n + 1)
                pe.wait_ge(x_placed, n + 1)
                for h in range(HALVES):
                    after(pe, cross_copied, HALVES * (n - 1) + h + 1)
                    for j in range(HB):
                        block_tx = tx[:, u % 2, HB * h + j]
                        mm = nc.tensor.matmul(pZ[h][:, BW * j:BW * (j + 1)], block_tx[:, 0:BT],
                                              block_tx, start=True, stop=True)
                    mm.then_inc(cross_done, 1)

            def link(q):
                pe.wait_ge(pairs_in, 80 * (q + 1))
                pe.wait_ge(pW_free, q + 1)
                for k in range(PAIR_TILES):
                    nc.tensor.matmul(pW[:, :], pairsT[:, k, :], wl_sb[:, k, :], start=k == 0, stop=False)
                nc.tensor.matmul(pW[:, :], extraT[0:XROWS, :], wx[:, :], start=False, stop=True).then_inc(linked, 1)

            def transpose_z(q):
                pe.wait_ge(z_ready, q + 1)
                for k in range(KZ):
                    mm = nc.tensor.transpose(pW[:, P * k:P * (k + 1)], zn[:, P * k:P * (k + 1)], eye_sb[:, :])
                mm.then_inc(z_transposed, 1)

            def top1(q):
                pe.wait_ge(hz_ready, q + 1)
                for c in range(K1):
                    for k in range(KTOP):
                        rhs = hz[:, k, :] if k < KZ else dense_sb[:, k - KZ, bass.ts(q, QB)]
                        mm = nc.tensor.matmul(pW[:, QB * c:QB * (c + 1)], w1_sb[:, k, P * c:P * (c + 1)], rhs,
                                              start=k == 0, stop=k == KTOP - 1)
                mm.then_inc(top1_done, 1)

            def top2(q):
                pe.wait_ge(h1_ready, q + 1)
                for c in range(K2):
                    for k in range(K1):
                        mm = nc.tensor.matmul(pW[:, QB * c:QB * (c + 1)], w2_sb[:, k, P * c:P * (c + 1)], h1[:, k, :],
                                              start=k == 0, stop=k == K1 - 1)
                mm.then_inc(top2_done, 1)

            def top3(q):
                pe.wait_ge(h2_ready, q + 1)
                for k in range(K2):
                    mm = nc.tensor.matmul(pW[0:1, 0:QB], w3_sb[:, k:k + 1], h2[:, k, :],
                                          start=k == 0, stop=k == K2 - 1)
                mm.then_inc(top3_done, 1)

            def step(i, s):
                if (at := unit(i, s, 0)):
                    stage_t(*at)
                if isinstance(i, int) and i == 0:
                    if s == 1:
                        pe.wait_ge(ws_steps, 3)
                    if s == 2:
                        prepare_mix()
                    if s == 5:
                        prepare_link()
                    if s == 6:
                        prepare_top()
                if (at := unit(i, s, LAG_Z)):
                    stage_z(*at)
                if quarter_step(i, s, SLOT_LINK):
                    link(i - 1)
                if quarter_step(i, s, SLOT_TRANSPOSE):
                    transpose_z(i - 1)
                if quarter_step(i, s, SLOT_TOP1):
                    top1(i - 1)
                if quarter_step(i, s, SLOT_TOP2):
                    top2(i - 1)
                if (at := unit(i, s, LAG_Y)):
                    stage_y(*at)
                if (at := unit(i, s, LAG_A)):
                    stage_a(*at)
                if quarter_step(i, s, SLOT_TOP3):
                    top3(i - 1)

            prepare()
            quarters(pe, step, UNITS - 1)

        @block.scalar
        def _(act):
            act.wait_ge(consts_ready, 1)
            act.wait_ge(x_stats, 2 * QUARTERS)
            act.activation(xstd[:, :], xmv[:, :, 1], ACT.Sqrt, bias=eps[:, :]).then_inc(x_std, 1)

            def make_sx():
                act.wait_ge(sx_made, 1)
                act.activation(sx[:, :], pW[0:1, :], ACT.Copy).then_inc(sx_ready, 1)

            def copy_embT(q, u):
                n = UNITS * q + u
                w = P * (CHUNKS[u][1] - CHUNKS[u][0])
                act.wait_ge(transposed, n + 1)
                after(act, projected, n - 1)
                act.activation(embT[:, u % 2, 0:w], pT[:, 0:w], ACT.Copy).then_inc(embT_ready, 1)

            def square1(q, u):
                n = UNITS * q + u
                w = 2 * (CHUNKS[u][1] - CHUNKS[u][0])
                act.wait_ge(projected, n + 1)
                after(act, summed1, n - 1)
                act.activation(sq1[:, u % 2, 0:w, :], pY[u % 2][:, 0:w * E].rearrange("p (t e) -> p t e", e=E),
                               ACT.Square).then_inc(squared1, 1)

            def root1(q, u):
                n = UNITS * q + u
                w = 2 * (CHUNKS[u][1] - CHUNKS[u][0])
                act.wait_ge(summed1, n + 1)
                after(act, rstd1_ready, n - 1)
                act.activation(std1[:, u % 2, 0:w], ss1[:, u % 2, 0:w], ACT.Sqrt, bias=eps[:, :],
                               scale=1.0 / E).then_inc(std1_ready, 1)

            def square2(q, u):
                n = UNITS * q + u
                act.wait_ge(y2_ready, n + 1)
                after(act, summed2, n - 1)
                act.activation(sq2[:, u % 2], y2[:, u % 2], ACT.Square).then_inc(squared2, 1)

            def root2(q, u):
                n = UNITS * q + u
                act.wait_ge(summed2, n + 1)
                after(act, rstd2_ready, n - 1)
                act.activation(std2[:, u % 2], ss2[:, u % 2], ACT.Sqrt, bias=eps[:, :],
                               scale=1.0 / PROJ).then_inc(std2_ready, 1)

            def copy_cross(q, u):
                n = UNITS * q + u
                for h in range(HALVES):
                    act.wait_ge(cross_done, HALVES * n + h + 1)
                    if u == 0 and h == 0:
                        after(act, pairs_out, 32 * BLOCK * q)
                    g = (UB // BLOCK) * u + HB * h
                    act.activation(crossed[:, :, g:g + HB].rearrange("p c g -> p g c"),
                                   pZ[h][:, 0:HB * BW].rearrange("p (g c) -> p g c", c=BW),
                                   ACT.Copy).then_inc(cross_copied, 1)

            def root_link(q):
                act.wait_ge(link_mean, q + 1)
                act.activation(wstd[:, :], wmv[:, 1:2], ACT.Sqrt, bias=eps[:, :]).then_inc(link_std, 1)

            def copy_hz(q):
                act.wait_ge(z_transposed, q + 1)
                act.activation(hz[:, :, :], pW[:, 0:KZ * QB].rearrange("p (k b) -> p k b", b=QB),
                               ACT.Copy).then_inc(hz_ready, 1)

            def relu1(q):
                act.wait_ge(top1_done, q + 1)
                act.wait_ge(pW_free, 1)
                for c in range(K1):
                    a = act.activation(h1[:, c, :], pW[:, QB * c:QB * (c + 1)], ACT.Relu, bias=bias1[:, c:c + 1])
                a.then_inc(h1_ready, 1)

            def relu2(q):
                act.wait_ge(top2_done, q + 1)
                for c in range(K2):
                    a = act.activation(h2[:, c, :], pW[:, QB * c:QB * (c + 1)], ACT.Relu, bias=b2_sb[:, c:c + 1])
                a.then_inc(h2_ready, 1)

            def step(i, s):
                if (at := unit(i, s, 0)):
                    copy_embT(*at)
                if isinstance(i, int) and i == 0 and s == 2:
                    make_sx()
                if (at := unit(i, s, LAG_Y)):
                    square1(*at)
                if quarter_step(i, s, SLOT_LINK):
                    root_link(i - 1)
                if quarter_step(i, s, SLOT_TRANSPOSE):
                    copy_hz(i - 1)
                if quarter_step(i, s, SLOT_TOP1):
                    relu1(i - 1)
                if quarter_step(i, s, SLOT_TOP2):
                    relu2(i - 1)
                if (at := unit(i, s, LAG_Z)):
                    copy_cross(*at)
                if (at := unit(i, s, LAG_Y)):
                    root1(*at)
                if (at := unit(i, s, LAG_A)):
                    square2(*at)
                    root2(*at)
            quarters(act, step, UNITS - 1)

        @block.vector
        def _(dve):
            V = nc.vector

            def prepare():
                V.memset(ones[:, :], 1.0)
                V.memset(tx[:, :, :, BW - 1:BW], 1.0)
                V.memset(extraT[2 * PROJ:3 * PROJ, :], 1.0)
                V.memset(eps[:, :], EPS).then_inc(consts_ready, 1)
                dve.wait_ge(ids_in, 32)
                V.tensor_tensor(rows_sb[:, :], ids_sb[:, :], bases_sb[:, :], ALU.add).then_inc(rows_ready, 1)
                dve.wait_ge(ws_in, 32)
                V.tensor_reduce(ws_mean[:, :], ws_sb[:, :, :], AX.X, ALU.add).then_inc(ws_steps, 1)
                dve.wait_ge(ws_steps, 1)
                V.tensor_scalar(ws_mean[:, :], ws_mean[:, :], 1.0 / E, None, ALU.mult).then_inc(ws_steps, 1)
                dve.wait_ge(ws_steps, 2)
                V.tensor_tensor(ws_sb[:, :, :], ws_sb[:, :, :], ws_mean[:, :, None].broadcast_to([P, 2, E]),
                                ALU.subtract).then_inc(ws_steps, 1)
                dve.wait_ge(x_projected, 1)
                for t in range(QUARTERS):
                    V.bn_stats(xstat[:, t, :], pW[:, E * t:E * (t + 1)]).then_inc(x_stats, 1)
                dve.wait_ge(x_stats, QUARTERS)
                for t in range(QUARTERS):
                    V.bn_aggr(xmv[:, t, :], xstat[:, t, :]).then_inc(x_stats, 1)
                dve.wait_ge(x_std, 1)
                V.reciprocal(xrstd[:, :], xstd[:, :]).then_inc(x_rstd, 1)
                dve.wait_ge(x_rstd, 1)
                dve.wait_ge(x_stats, 2 * QUARTERS)
                for t in range(QUARTERS):
                    v = V.tensor_scalar(xn[:, t, :], pW[:, E * t:E * (t + 1)], xmv[:, t, 0:1], xrstd[:, t:t + 1],
                                        ALU.subtract, ALU.mult)
                v.then_inc(x_normed, 1)
                dve.wait_ge(mix_in, 48)
                V.tensor_reduce(mix_mean[:, :], mix_sb[:, :, :], AX.X, ALU.add).then_inc(mix_steps, 1)
                dve.wait_ge(mix_steps, 1)
                V.tensor_scalar(mix_mean[:, :], mix_mean[:, :], 1.0 / PROJ, None, ALU.mult).then_inc(mix_steps, 1)
                dve.wait_ge(x_transposed, 1)
                dve.wait_ge(dense_in, 64)
                V.tensor_scalar(xT[:, :, :, :].rearrange("e q b g -> e (q b g)"), pA[0][:, :], gd_sb[:, :], bd_sb[:, :],
                                ALU.mult, ALU.add).then_inc(x_ready, 1)
                dve.wait_ge(mix_steps, 2)
                V.tensor_tensor(mix_sb[:, :, :], mix_sb[:, :, :],
                                mix_mean[:, :, None].broadcast_to([P, MIX_COLS // PROJ, PROJ]),
                                ALU.subtract).then_inc(mix_steps, 1)

            def make_shift():
                dve.wait_ge(shift_made, 1)
                V.tensor_copy(shift[:, :], pW[:, 0:PROJ]).then_inc(shift_ready, 1)

            def fold_link():
                dve.wait_ge(wl_in, 112)
                V.tensor_tensor(gg[:, :], gpq_sb[:, 0, :], gpq_sb[:, 1, :], ALU.mult).then_inc(gg_ready, 1)
                V.scalar_tensor_tensor(fold_sb[:, :, XROWS - 1], bpq_sb[:, 0, :], float(E), bpq_sb[:, 1, :],
                                       ALU.mult, ALU.mult).then_inc(fold_ready, 1)

            def scale_link():
                dve.wait_ge(wx_made, 1)
                V.tensor_scalar(wx[:, :], pW[0:XROWS, :], xscale_sb[:, :], None, ALU.mult).then_inc(wx_ready, 1)
                dve.wait_ge(gg_ready, 1)
                for k in range(PAIR_TILES):
                    V.tensor_scalar(wl_sb[:, k, :], wl_sb[:, k, :], gg[:, k:k + 1], None,
                                    ALU.mult).then_inc(wl_ready, 1)

            def scale_top():
                dve.wait_ge(bias1_made, 1)
                dve.wait_ge(top_in, 112)
                V.tensor_tensor(bias1[:, :], pW[:, 0:K1], b1_sb[:, :], ALU.add).then_inc(pW_free, 1)
                for k in range(KZ):
                    V.tensor_scalar(w1_sb[:, k, :], w1_sb[:, k, :], gl_sb[:, k:k + 1], None,
                                    ALU.mult).then_inc(w1_ready, 1)

            def sum1(q, u):
                n = UNITS * q + u
                w = 2 * (CHUNKS[u][1] - CHUNKS[u][0])
                dve.wait_ge(squared1, n + 1)
                after(dve, std1_ready, n - 1)
                V.tensor_reduce(ss1[:, u % 2, 0:w], sq1[:, u % 2, 0:w, :], AX.X, ALU.add).then_inc(summed1, 1)

            def invert1(q, u):
                n = UNITS * q + u
                w = 2 * (CHUNKS[u][1] - CHUNKS[u][0])
                dve.wait_ge(std1_ready, n + 1)
                after(dve, yn_ready, n - 1)
                V.reciprocal(rstd1[:, u % 2, 0:w], std1[:, u % 2, 0:w]).then_inc(rstd1_ready, 1)

            def norm1(q, u):
                n = UNITS * q + u
                lo, hi = 2 * CHUNKS[u][0], 2 * CHUNKS[u][1]
                w = hi - lo
                dve.wait_ge(rstd1_ready, n + 1)
                after(dve, mixed, n - UNITS + 2)
                V.tensor_tensor(yn[:, lo:hi, :], pY[u % 2][:, 0:w * E].rearrange("p (t e) -> p t e", e=E),
                                rstd1[:, u % 2, 0:w, None].broadcast_to([P, w, E]), ALU.mult).then_inc(yn_ready, 1)

            def affine2(q, u):
                n = UNITS * q + u
                dve.wait_ge(mixed, n + 1)
                after(dve, squared2, n - 1)
                after(dve, t_ready, n - 1)
                V.scalar_tensor_tensor(y2[:, u % 2], pA[u % 2][:, :].rearrange("e (b c) -> e b c", c=PROJ),
                                       gs_sb[:, :], shift[:, None, :].broadcast_to([E, UB, PROJ]),
                                       ALU.mult, ALU.add).then_inc(y2_ready, 1)

            def sum2(q, u):
                n = UNITS * q + u
                dve.wait_ge(squared2, n + 1)
                after(dve, std2_ready, n - 1)
                V.tensor_reduce(ss2[:, u % 2], sq2[:, u % 2], AX.X, ALU.add).then_inc(summed2, 1)

            def invert2(q, u):
                n = UNITS * q + u
                dve.wait_ge(std2_ready, n + 1)
                after(dve, t_ready, n - 1)
                V.reciprocal(rstd2[:, u % 2], std2[:, u % 2]).then_inc(rstd2_ready, 1)

            def place_x(q, u):
                n = UNITS * q + u
                after(dve, cross_done, HALVES * (n - 1))
                g = (UB // BLOCK) * u
                V.tensor_copy(tx[:, u % 2, :, BT:BT + BLOCK],
                              xT[:, q, :, g:g + UB // BLOCK].rearrange("e b g -> e g b")
                              if isinstance(q, int) else
                              xT[:, bass.ds(q, 1), :, g:g + UB // BLOCK].rearrange("e o b g -> e (o g) b")
                              ).then_inc(x_placed, 1)

            def norm2(q, u):
                n = UNITS * q + u
                dve.wait_ge(rstd2_ready, n + 1)
                V.tensor_tensor(tx[:, u % 2, :, 0:BT].rearrange("e g (b c) -> e g b c", b=BLOCK),
                                y2[:, u % 2].rearrange("e (g b) c -> e g b c", b=BLOCK),
                                rstd2[:, u % 2].rearrange("e (g b) -> e g b", b=BLOCK)[:, :, :, None]
                                .broadcast_to([E, UB // BLOCK, BLOCK, PROJ]), ALU.mult).then_inc(t_ready, 1)

            def link_norm(q):
                dve.wait_ge(linked, q + 1)
                V.bn_stats(wstat[:, :], pW[:, :]).then_inc(link_stats, 1)
                dve.wait_ge(consts_ready, 1)
                dve.wait_ge(link_stats, q + 1)
                V.bn_aggr(wmv[:, :], wstat[:, :]).then_inc(link_mean, 1)
                dve.wait_ge(link_std, q + 1)
                V.reciprocal(wrstd[:, :], wstd[:, :]).then_inc(link_rstd, 1)
                dve.wait_ge(link_rstd, q + 1)
                V.tensor_scalar(zn[:, :], pW[:, 0:DIMS_IN_USE], wmv[:, 0:1], wrstd[:, :],
                                ALU.subtract, ALU.mult).then_inc(z_ready, 1)

            def copy_y(q):
                dve.wait_ge(top3_done, q + 1)
                y_q = y_all[:, q, :] if isinstance(q, int) else y_all[:, bass.ds(q, 1), :].rearrange("o q b -> o (q b)")
                V.tensor_scalar(y_q, pW[0:1, 0:QB], 1.0, None, ALU.mult).then_inc(pW_free, 1)

            def step(i, s):
                if (at := unit(i, s, LAG_Z)):
                    invert2(*at)
                    place_x(*at)
                    norm2(*at)
                if isinstance(i, int) and i == 0:
                    if s == 2:
                        make_shift()
                    if s == 4:
                        fold_link()
                    if s == 6:
                        scale_link()
                        scale_top()
                if (at := unit(i, s, LAG_Y)):
                    sum1(*at)
                if quarter_step(i, s, SLOT_LINK):
                    link_norm(i - 1)
                if (at := unit(i, s, LAG_A)):
                    affine2(*at)
                if (at := unit(i, s, LAG_Y)):
                    invert1(*at)
                    norm1(*at)
                if (at := unit(i, s, LAG_A)):
                    sum2(*at)
                if quarter_step(i, s, SLOT_TOP3):
                    copy_y(i - 1)

            prepare()
            quarters(dve, step, UNITS - 1)


def kernel(**inputs):
    import concourse.bacc as bacc
    from concourse.bass_utils import run_bass_kernel_spmd

    a = {name: np.asarray(value) for name, value in inputs.items()}
    tables = [a[f"tbl_{n}"] for n in range(N_SPARSE)]
    f32 = a["W_top1"].dtype

    starts = np.cumsum([0] + [t.shape[0] for t in tables[:-1]]).astype(np.int32)
    bases = np.tile(starts, BATCH).reshape(QUARTERS * TILES, P).T
    ids = a["ids"].reshape(QUARTERS * TILES, P).T

    ws = np.zeros((P, 2, E), f32)
    ws[:D_SPARSE, 0] = ws[D_SPARSE:, 1] = a["L0_rec_Ws"].T

    wmix = np.zeros((P, MIX_COLS // PROJ, PROJ), f32)
    for u, segs in enumerate(MIX):
        for t, first, count, col in segs:
            for b in range(count):
                for n in range(N_SPARSE):
                    r = (UB * u + first + b) * N_SPARSE + n - t * P
                    if 0 <= r < P:
                        wmix[r, col // PROJ + b] = a["L0_rec_Wsi"][:, n]

    dense = a["r_dense_t"].reshape(QUARTERS, GROUPS, BLOCK, KD, P).transpose(4, 3, 0, 2, 1).reshape(P, KD, BATCH)
    wd = a["L0_rec_Wd"].T.reshape(KD, P, E).transpose(1, 0, 2)

    wl = np.zeros((PAIR_TILES * P, MAXD), f32)
    gpq = np.zeros((2, PAIR_TILES * P), f32)
    bpq = np.zeros((2, PAIR_TILES * P), f32)
    fold = np.zeros((PAIR_TILES * P, XROWS), f32)
    g, b = a["L0_rec_gsi"], a["L0_rec_bsi"]
    for r, (p, q) in enumerate(pair_rows()):
        if p > q:
            wl[r] = a["L0_rec_Wl"][:, (p + 1) * p // 2 + q + 1]
            gpq[:, r] = g[p], g[q]
            bpq[:, r] = b[p], b[q]
            fold[r, PROJ + p], fold[r, PROJ + q] = b[q], b[p]
    wlx = a["L0_rec_Wl"][:, [(p + 1) * p // 2 for p in range(PROJ)]].T
    foldx = np.zeros((PROJ, XROWS), f32)
    foldx[np.arange(PROJ), np.arange(PROJ)] = 1
    foldx[:, 2 * PROJ] = b
    xscale = np.concatenate([g, g, np.ones(2, f32)])[:, None]

    def k_tiles(w):
        return w.reshape(-1, P, *w.shape[1:]).swapaxes(0, 1)

    arrays = {
        "tables": np.concatenate(tables), "ids": ids, "bases": bases, "eye": np.eye(P, dtype=f32), "ws": ws,
        "wmix": wmix, "gs": a["L0_rec_gs"][:, None], "bs": a["L0_rec_bs"][None, :], "dense": dense, "wd": wd,
        "gd": a["L0_rec_gd"][:, None], "bd": a["L0_rec_bd"][:, None], "wl": k_tiles(wl), "wlx": wlx,
        "gpq": gpq.reshape(2, PAIR_TILES, P).transpose(2, 0, 1), "bpq": bpq.reshape(2, PAIR_TILES, P).transpose(2, 0, 1),
        "fold": k_tiles(fold), "foldx": foldx, "xscale": xscale,
        "w1": k_tiles(np.concatenate([a["W_top1"][:DIMS_IN_USE], a["W_top1"][MAXD:]])),
        "b1": k_tiles(a["b_top1"]), "w2": k_tiles(a["W_top2"]), "b2": k_tiles(a["b_top2"]),
        "w3": k_tiles(a["W_top3"])[:, :, 0],
        "gl": k_tiles(a["L0_rec_gl"][:DIMS_IN_USE]), "bl": k_tiles(a["L0_rec_bl"][:DIMS_IN_USE]),
    }
    arrays = {f"in_{k}": np.ascontiguousarray(v) for k, v in arrays.items()}

    nc = bacc.Bacc("TRN2", target_bir_lowering=False, num_devices=1)
    args = [nc.dram_tensor(k, v.shape, mybir.dt.from_np(v.dtype), kind="ExternalInput").ap() for k, v in arrays.items()]
    out = nc.dram_tensor("out_y", (1, QUARTERS, QB), mybir.dt.float32, kind="ExternalOutput").ap()
    tower(nc, *args, out)
    r = run_bass_kernel_spmd(nc, [arrays], core_ids=[0])
    y = np.asarray(r.results[0]["out_y"])
    return y.reshape(QUARTERS, BLOCK, GROUPS).transpose(0, 2, 1).reshape(BATCH, 1)
```

```python
from contextlib import ExitStack

import concourse.bass as bass
import numpy as np
from concourse import mybir

P = 128
BATCH, N_SPARSE, D_SPARSE, D_DENSE = 512, 26, 64, 256
E, PROJ, MAXD, DIMS_IN_USE = 128, 32, 512, 384
H1, H2 = 512, 256
EPS = 1e-5

QUARTERS = 4
QB = BATCH // QUARTERS
UNITS = 8
UB = QB // UNITS
TILES = QB * N_SPARSE // P
PERIOD = TILES // 2
BLOCK = 4
GROUPS = QB // BLOCK
BT = BLOCK * PROJ
BW = BT + BLOCK + 1
HALVES = 2
HB = UB // BLOCK // HALVES
KD = D_DENSE // P
KZ = DIMS_IN_USE // P
KTOP = KZ + KD
K1, K2 = H1 // P, H2 // P
XROWS = 2 * PROJ + 2
QT = P // PROJ
PAIR_TILES = PROJ // QT
RELAY = 2


def chunk_pairs():
    need = [-(-(UB * N_SPARSE * (u + 1)) // (2 * P)) for u in range(UNITS)]
    return [(a, b) for a, b in zip([0] + need[:-1], need)]


def segments():
    out, col = [], 0
    for u in range(UNITS // 2):
        segs = []
        lo, hi = UB * u, UB * (u + 1)
        for t in range(PERIOD):
            first = max(lo, t * P // N_SPARSE)
            last = min(hi - 1, (t * P + P - 1) // N_SPARSE)
            if first <= last:
                segs.append((t, first - lo, last - first + 1, col))
                col += (last - first + 1) * PROJ
        out.append(segs)
    return out, col


CHUNKS = chunk_pairs()
MIX, MIX_COLS = segments()


def mix_part(u):
    return MIX[u][0][3] // PROJ, (MIX[u + 1][0][3] if u + 1 < len(MIX) else MIX_COLS) // PROJ


def pair_rows():
    return [(k % PROJ, QT * kt + k // PROJ) for kt in range(PAIR_TILES) for k in range(P)]


def tower(nc, tables, ids, bases, eye, ws, wmix, gs, bs, dense, wd, gd, bd, wl, wlx, gpq, bpq, fold, foldx, xscale,
          w1, b1, w2, b2, w3, gl, bl, out):
    f32, i32 = mybir.dt.float32, mybir.dt.int32
    ALU, ACT, AX = mybir.AluOpType, mybir.ActivationFunctionType, mybir.AxisListType

    ctx = ExitStack()
    with ctx:
        def sb(name, shape, dt=f32):
            return ctx.enter_context(nc.sbuf_tensor(name, shape, dt))

        def bank(name):
            return ctx.enter_context(nc.psum_tensor(name, [P, 512], f32))

        def sem(name):
            return ctx.enter_context(nc.semaphore(name))

        ids_sb = sb("ids_sb", [P, QUARTERS * TILES], i32)
        bases_sb = sb("bases_sb", [P, QUARTERS * TILES], i32)
        rows_sb = sb("rows_sb", [P, QUARTERS * TILES], i32)
        eye_sb = sb("eye_sb", [P, P])
        emb = sb("emb", [P, TILES, D_SPARSE])
        embT = sb("embT", [P, 2, 2 * P])
        ws_sb = sb("ws_sb", [P, 2, E])
        ws_mean = sb("ws_mean", [P, 2])
        sq1 = sb("sq1", [P, 2, 4, E])
        ss1 = sb("ss1", [P, 2, 4])
        std1 = sb("std1", [P, 2, 4])
        rstd1 = sb("rstd1", [P, 2, 4])
        yn = sb("yn", [P, TILES, E])
        mix_sb = sb("mix_sb", [P, MIX_COLS // PROJ, PROJ])
        mix_mean = sb("mix_mean", [P, MIX_COLS // PROJ])
        gs_sb = sb("gs_sb", [E, 1])
        bs_rep = sb("bs_rep", [N_SPARSE, E])
        shift = sb("shift", [E, PROJ])
        y2 = sb("y2", [E, 2, UB, PROJ])
        sq2 = sb("sq2", [E, 2, UB, PROJ])
        ss2 = sb("ss2", [E, 2, UB])
        std2 = sb("std2", [E, 2, UB])
        rstd2 = sb("rstd2", [E, 2, UB])
        tx = sb("tx", [E, 2, UB // BLOCK, BW])
        crossed = sb("crossed", [P, BW, GROUPS])
        pairsT = sb("pairsT", [P, PAIR_TILES, QB])
        extraT = sb("extraT", [P, QB])
        dense_sb = sb("dense_sb", [P, KD, BATCH])
        wd_sb = sb("wd_sb", [P, KD, E])
        gd_sb = sb("gd_sb", [E, 1])
        bd_sb = sb("bd_sb", [E, 1])
        xstat = sb("xstat", [P, QUARTERS, 6])
        xmv = sb("xmv", [P, QUARTERS, 2])
        xstd = sb("xstd", [P, QUARTERS])
        xrstd = sb("xrstd", [P, QUARTERS])
        xn = sb("xn", [P, QUARTERS, E])
        xT = sb("xT", [E, QUARTERS, BLOCK, GROUPS])
        sx = sb("sx", [1, BATCH])
        ones = sb("ones", [P, 1])
        eps = sb("eps", [P, 1])
        wl_sb = sb("wl_sb", [P, PAIR_TILES, MAXD])
        wlx_sb = sb("wlx_sb", [PROJ, MAXD])
        wx = sb("wx", [XROWS, MAXD])
        gpq_sb = sb("gpq_sb", [P, 2, PAIR_TILES])
        bpq_sb = sb("bpq_sb", [P, 2, PAIR_TILES])
        gg = sb("gg", [P, PAIR_TILES])
        fold_sb = sb("fold_sb", [P, PAIR_TILES, XROWS])
        foldx_sb = sb("foldx_sb", [PROJ, XROWS])
        xscale_sb = sb("xscale_sb", [XROWS, 1])
        w1_sb = sb("w1_sb", [P, KTOP, H1])
        b1_sb = sb("b1_sb", [P, K1])
        bias1 = sb("bias1", [P, K1])
        w2_sb = sb("w2_sb", [P, K1, H2])
        b2_sb = sb("b2_sb", [P, K2])
        w3_sb = sb("w3_sb", [P, K2])
        gl_sb = sb("gl_sb", [P, KZ])
        bl_sb = sb("bl_sb", [P, KZ])
        wstat = sb("wstat", [P, 6])
        wmv = sb("wmv", [P, 2])
        wstd = sb("wstd", [P, 1])
        wrstd = sb("wrstd", [P, 1])
        zn = sb("zn", [P, DIMS_IN_USE])
        hz = sb("hz", [P, KZ, QB])
        h1 = sb("h1", [P, K1, QB])
        h2 = sb("h2", [P, K2, QB])
        y_all = sb("y_all", [1, QUARTERS, QB])

        pT = bank("pT")
        pY = [bank("pY0"), bank("pY1")]
        pA = [bank("pA0"), bank("pA1")]
        pZ = [bank("pZ0"), bank("pZ1")]
        pW = bank("pW")

        ids_in = sem("ids_in")
        ws_in = sem("ws_in")
        dense_in = sem("dense_in")
        mix_in = [sem(f"mix_in{u}") for u in range(len(MIX))]
        gsbs_in = sem("gsbs_in")
        wl_in = sem("wl_in")
        top_in = sem("top_in")
        rows_ready = sem("rows_ready")
        consts_ready = sem("consts_ready")
        ws_steps = sem("ws_steps")
        mix_steps = sem("mix_steps")
        mix_ready = sem("mix_ready")
        x_projected = sem("x_projected")
        x_stats = sem("x_stats")
        x_std = sem("x_std")
        x_rstd = sem("x_rstd")
        x_normed = sem("x_normed")
        x_transposed = sem("x_transposed")
        x_ready = sem("x_ready")
        shift_made = sem("shift_made")
        shift_ready = sem("shift_ready")
        sx_made = sem("sx_made")
        sx_ready = sem("sx_ready")
        gg_ready = sem("gg_ready")
        fold_ready = sem("fold_ready")
        wx_made = sem("wx_made")
        wx_ready = sem("wx_ready")
        wl_ready = sem("wl_ready")
        bias1_made = sem("bias1_made")
        w1_ready = sem("w1_ready")
        gathered = [sem(f"gathered{u}") for u in range(UNITS)]
        transposed = sem("transposed")
        embT_ready = sem("embT_ready")
        projected = sem("projected")
        summed1 = sem("summed1")
        std1_ready = sem("std1_ready")
        rstd1_ready = sem("rstd1_ready")
        yn_ready = sem("yn_ready")
        mixed = sem("mixed")
        y2_ready = sem("y2_ready")
        squared2 = sem("squared2")
        summed2 = sem("summed2")
        std2_ready = sem("std2_ready")
        rstd2_ready = sem("rstd2_ready")
        x_placed = sem("x_placed")
        t_ready = sem("t_ready")
        cross_done = sem("cross_done")
        cross_copied = sem("cross_copied")
        relaid = sem("relaid")
        linked = sem("linked")
        link_stats = sem("link_stats")
        link_mean = sem("link_mean")
        link_std = sem("link_std")
        link_rstd = sem("link_rstd")
        z_ready = sem("z_ready")
        z_transposed = sem("z_transposed")
        hz_ready = sem("hz_ready")
        top1_done = sem("top1_done")
        h1_ready = sem("h1_ready")
        top2_done = sem("top2_done")
        h2_ready = sem("h2_ready")
        top3_done = sem("top3_done")
        pW_free = sem("pW_free")
        y_out = sem("y_out")

        def after(eng, semaphore, value):
            if not (isinstance(value, int) and value <= 0):
                eng.wait_ge(semaphore, value)

        def run_rounds(eng, step):
            for i in (0, 1):
                for s in range(UNITS):
                    step(i, s)
            with eng.Fori(2, QUARTERS) as i:
                for s in range(UNITS):
                    step(i, s)
            for i in (QUARTERS, QUARTERS + 1):
                for s in range(UNITS):
                    step(i, s)

        def unit(i, s, lag):
            q, u = (i, s - lag) if s >= lag else (i - 1, s - lag + UNITS)
            if isinstance(i, int) and (q < 0 or q >= QUARTERS):
                return None
            return q, u

        def quarter(i, s, when):
            if s != when[1] or isinstance(i, int) and not 0 <= i - when[0] < QUARTERS:
                return None
            return (i - when[0],)

        LAG_Y, LAG_YN, LAG_A, LAG_Y2, LAG_T, LAG_Z = 1, 2, 2, 3, 4, 5
        RELAYS = [((1, 2), 0, (0, 1)), ((1, 3), 0, (2, 3)), ((1, 5), 1, (0, 1)), ((1, 6), 1, (2, 3))]
        LINKS = [((1, 7), 0, 3), ((2, 0), 3, 6), ((2, 1), 6, PAIR_TILES + 1)]
        LINKED = LINKS[-1][0]
        TRANSPOSE = (2, 2)
        TOP1 = [((2, 3), 0, K1 // 2), ((2, 4), K1 // 2, K1)]
        TOP2 = (2, 5)
        TOP3 = (2, 6)

        block = ctx.enter_context(nc.Block())

        @block.gpsimd
        def _(pool):
            pool.wait_ge(rows_ready, 1)
            for q in range(QUARTERS):
                for u in range(UNITS):
                    lo, hi = 2 * CHUNKS[u][0], 2 * CHUNKS[u][1]
                    after(pool, transposed, UNITS * (q - 1) + u + 1)
                    for t in range(lo, hi):
                        c = q * TILES + t
                        nc.gpsimd.indirect_dma_start(
                            emb[:, t, :], None, tables[:, :],
                            bass.IndirectOffsetOnAxis(rows_sb[:, c:c + 1], 0)).then_inc(gathered[u], 16)

        @block.sync
        def _(sp):
            sp.dma_start(ids_sb[:, :], ids).then_inc(ids_in, 16)
            sp.dma_start(bases_sb[:, :], bases).then_inc(ids_in, 16)
            sp.dma_start(ws_sb[:, :, :], ws).then_inc(ws_in, 16)
            sp.dma_start(eye_sb[:, :], eye).then_inc(ws_in, 16)
            def load_mix(u):
                lo, hi = mix_part(u)
                sp.dma_start(mix_sb[:, lo:hi, :], wmix[:, lo:hi, :]).then_inc(mix_in[u], 16)

            load_mix(0)
            sp.dma_start(gs_sb[:, :], gs).then_inc(gsbs_in, 16)
            sp.dma_start(bs_rep[:, :], bs.broadcast_to([N_SPARSE, E])).then_inc(gsbs_in, 16)
            sp.wait_ge(gathered[0], 16 * 4)
            load_mix(1)
            sp.dma_start(dense_sb[:, :, :], dense).then_inc(dense_in, 16)
            sp.dma_start(wd_sb[:, :, :], wd).then_inc(dense_in, 16)
            sp.dma_start(gd_sb[:, :], gd).then_inc(dense_in, 16)
            sp.dma_start(bd_sb[:, :], bd).then_inc(dense_in, 16)
            sp.wait_ge(gathered[1], 16 * 4)
            load_mix(2)
            load_mix(3)
            sp.wait_ge(gathered[2], 16 * 2)
            for k in range(0, PAIR_TILES, 2):
                sp.dma_start(wl_sb[:, k:k + 2, :], wl[:, k:k + 2, :]).then_inc(wl_in, 16)
                sp.wait_ge(wl_in, 8 * (k + 2))
            sp.dma_start(wlx_sb[:, :], wlx).then_inc(wl_in, 16)
            sp.dma_start(gpq_sb[:, :, :], gpq).then_inc(wl_in, 16)
            sp.dma_start(bpq_sb[:, :, :], bpq).then_inc(wl_in, 16)
            sp.dma_start(fold_sb[:, :, :], fold).then_inc(wl_in, 16)
            sp.dma_start(foldx_sb[:, :], foldx).then_inc(wl_in, 16)
            sp.dma_start(xscale_sb[:, :], xscale).then_inc(wl_in, 16)
            sp.wait_ge(gathered[4], 16 * 4)
            sp.dma_start(b1_sb[:, :], b1).then_inc(top_in, 16)
            sp.dma_start(w1_sb[:, :, :], w1).then_inc(top_in, 16)
            sp.wait_ge(gathered[5], 16 * 2)
            sp.dma_start(w2_sb[:, :, :], w2).then_inc(top_in, 16)
            sp.dma_start(b2_sb[:, :], b2).then_inc(top_in, 16)
            sp.dma_start(w3_sb[:, :], w3).then_inc(top_in, 16)
            sp.dma_start(gl_sb[:, :], gl).then_inc(top_in, 16)
            sp.dma_start(bl_sb[:, :], bl).then_inc(top_in, 16)
            sp.wait_ge(pW_free, QUARTERS + 1)
            sp.dma_start(out, y_all[:, :, :]).then_inc(y_out, 16)
            sp.wait_ge(y_out, 16)

        @block.tensor
        def _(pe):
            def project_x():
                pe.wait_ge(dense_in, 64)
                for t in range(QUARTERS):
                    for k in range(KD):
                        mm = nc.tensor.matmul(pW[:, E * t:E * (t + 1)], dense_sb[:, k, P * t:P * (t + 1)],
                                              wd_sb[:, k, :], start=k == 0, stop=k == KD - 1)
                mm.then_inc(x_projected, 1)

            def prepare_shift():
                pe.wait_ge(mix_ready, 1)
                pe.wait_ge(gsbs_in, 32)
                nc.tensor.matmul(pZ[0][:, 0:PROJ], bs_rep[:, :], mix_sb[0:N_SPARSE, 0, :],
                                 start=True, stop=True).then_inc(shift_made, 1)

            def transpose_x():
                pe.wait_ge(x_normed, 1)
                for t in range(QUARTERS):
                    mm = nc.tensor.transpose(pZ[1][:, P * t:P * (t + 1)], xn[:, t, :], eye_sb[:, :])
                mm.then_inc(x_transposed, 1)

            def sum_x():
                pe.wait_ge(shift_ready, 1)
                pe.wait_ge(x_ready, 1)
                nc.tensor.matmul(pZ[0][0:1, :], ones[:, :], xT[:, :, :, :].rearrange("e q b g -> e (q b g)"),
                                 start=True, stop=True).then_inc(sx_made, 1)

            def prepare_link():
                pe.wait_ge(fold_ready, 1)
                for k in range(PAIR_TILES):
                    nc.tensor.matmul(pW[0:XROWS, :], fold_sb[:, k, :], wl_sb[:, k, :], start=k == 0, stop=False)
                nc.tensor.matmul(pW[0:XROWS, :], foldx_sb[:, :], wlx_sb[:, :],
                                 start=False, stop=True).then_inc(wx_made, 1)

            def prepare_top():
                pe.wait_ge(top_in, 112)
                pe.wait_ge(wx_ready, 1)
                for c in range(K1):
                    for k in range(KZ):
                        mm = nc.tensor.matmul(pW[:, c:c + 1], w1_sb[:, k, P * c:P * (c + 1)], bl_sb[:, k:k + 1],
                                              start=k == 0, stop=k == KZ - 1)
                mm.then_inc(bias1_made, 1)

            def stage_t(q, u):
                n = UNITS * q + u
                lo, hi = CHUNKS[u]
                pe.wait_ge(gathered[u], 32 * (hi - lo) * (q + 1))
                after(pe, embT_ready, n)
                for j in range(lo, hi):
                    mm = nc.tensor.transpose(pT[:, P * (j - lo):P * (j - lo + 1)],
                                             emb[:, 2 * j:2 * j + 2, :].rearrange("p t d -> p (t d)"), eye_sb[:, :])
                mm.then_inc(transposed, 1)

            def stage_y(q, u):
                n = UNITS * q + u
                lo, hi = CHUNKS[u]
                pe.wait_ge(embT_ready, n + 1)
                after(pe, yn_ready, n - 1)
                for j in range(hi - lo):
                    mm = nc.tensor.matmul(pY[u % 2][:, 2 * E * j:2 * E * (j + 1)], embT[:, u % 2, P * j:P * (j + 1)],
                                          ws_sb[:, :, :].rearrange("p t e -> p (t e)"), start=True, stop=True)
                mm.then_inc(projected, 1)

            def stage_a(q, u):
                n = UNITS * q + u
                pe.wait_ge(yn_ready, n + 1)
                if isinstance(q, int) and q == 0 and u < len(MIX):
                    pe.wait_ge(mix_ready, u + 1)
                after(pe, y2_ready, n - 1)
                segs = MIX[u % len(MIX)]
                for t, first, count, col in segs:
                    tile = PERIOD * (u // len(MIX)) + t
                    mm = nc.tensor.matmul(
                        pA[u % 2][:, PROJ * first:PROJ * (first + count)], yn[:, tile, :],
                        mix_sb[:, col // PROJ:col // PROJ + count, :].rearrange("p b c -> p (b c)"),
                        start=t == segs[0][0], stop=t == segs[-1][0], skip_group_check=True)
                mm.then_inc(mixed, 1)

            def stage_z(q, u):
                n = UNITS * q + u
                pe.wait_ge(t_ready, n + 1)
                pe.wait_ge(x_placed, n + 1)
                if isinstance(q, int) and n == 0:
                    pe.wait_ge(sx_ready, 1)
                for h in range(HALVES):
                    after(pe, cross_copied, HALVES * (n - 1) + h + 1)
                    for j in range(HB):
                        block_tx = tx[:, u % 2, HB * h + j]
                        mm = nc.tensor.matmul(pZ[h][:, BW * j:BW * (j + 1)], block_tx[:, 0:BT],
                                              block_tx, start=True, stop=True)
                    mm.then_inc(cross_done, 1)

            def link(q, lo, hi):
                if lo == 0:
                    pe.wait_ge(relaid, RELAY * (q + 1) + 1)
                    pe.wait_ge(pW_free, q + 1)
                for k in range(lo, min(hi, PAIR_TILES)):
                    nc.tensor.matmul(pW[:, :], pairsT[:, k, :], wl_sb[:, k, :], start=k == 0, stop=False)
                if hi > PAIR_TILES:
                    nc.tensor.matmul(pW[:, :], extraT[0:XROWS, :], wx[:, :],
                                     start=False, stop=True).then_inc(linked, 1)

            def transpose_z(q):
                pe.wait_ge(z_ready, q + 1)
                for k in range(KZ):
                    mm = nc.tensor.transpose(pW[:, P * k:P * (k + 1)], zn[:, P * k:P * (k + 1)], eye_sb[:, :])
                mm.then_inc(z_transposed, 1)

            def top1(q, lo, hi):
                pe.wait_ge(hz_ready, q + 1)
                for c in range(lo, hi):
                    for k in range(KTOP):
                        rhs = hz[:, k, :] if k < KZ else dense_sb[:, k - KZ, bass.ts(q, QB)]
                        mm = nc.tensor.matmul(pW[:, QB * c:QB * (c + 1)], w1_sb[:, k, P * c:P * (c + 1)], rhs,
                                              start=k == 0, stop=k == KTOP - 1)
                if hi == K1:
                    mm.then_inc(top1_done, 1)

            def top2(q):
                pe.wait_ge(h1_ready, q + 1)
                for c in range(K2):
                    for k in range(K1):
                        mm = nc.tensor.matmul(pW[:, QB * c:QB * (c + 1)], w2_sb[:, k, P * c:P * (c + 1)], h1[:, k, :],
                                              start=k == 0, stop=k == K1 - 1)
                mm.then_inc(top2_done, 1)

            def top3(q):
                pe.wait_ge(h2_ready, q + 1)
                for k in range(K2):
                    mm = nc.tensor.matmul(pW[0:1, 0:QB], w3_sb[:, k:k + 1], h2[:, k, :],
                                          start=k == 0, stop=k == K2 - 1)
                mm.then_inc(top3_done, 1)

            def step(i, s):
                first = isinstance(i, int) and i == 0
                if (at := unit(i, s, LAG_Z)):
                    stage_z(*at)
                if (at := unit(i, s, 0)):
                    stage_t(*at)
                if first and s == 1:
                    pe.wait_ge(ws_steps, 3)
                if (at := unit(i, s, LAG_Y)):
                    stage_y(*at)
                if (at := quarter(i, s, TRANSPOSE)):
                    transpose_z(*at)
                for when, lo, hi in LINKS:
                    if (at := quarter(i, s, when)):
                        link(*at, lo, hi)
                for when, lo, hi in TOP1:
                    if (at := quarter(i, s, when)):
                        top1(*at, lo, hi)
                if (at := quarter(i, s, TOP2)):
                    top2(*at)
                if (at := quarter(i, s, TOP3)):
                    top3(*at)
                if first and s == 1:
                    project_x()
                    prepare_shift()
                if first and s == 2:
                    transpose_x()
                if first and s == 3:
                    sum_x()
                if (at := unit(i, s, LAG_A)):
                    stage_a(*at)
                if first and s == 6:
                    prepare_link()
                if first and s == 7:
                    prepare_top()

            pe.wait_ge(ws_in, 32)
            run_rounds(pe, step)

        @block.scalar
        def _(act):
            def root_x():
                act.wait_ge(x_stats, 2 * QUARTERS)
                act.activation(xstd[:, :], xmv[:, :, 1], ACT.Sqrt, bias=eps[:, :]).then_inc(x_std, 1)

            def make_sx():
                act.wait_ge(sx_made, 1)
                act.activation(sx[:, :], pZ[0][0:1, :], ACT.Copy).then_inc(sx_ready, 1)

            def copy_embT(q, u):
                n = UNITS * q + u
                w = P * (CHUNKS[u][1] - CHUNKS[u][0])
                act.wait_ge(transposed, n + 1)
                after(act, projected, n - 1)
                act.activation(embT[:, u % 2, 0:w], pT[:, 0:w], ACT.Copy).then_inc(embT_ready, 1)

            def square1(q, u):
                n = UNITS * q + u
                w = 2 * (CHUNKS[u][1] - CHUNKS[u][0])
                act.wait_ge(projected, n + 1)
                after(act, std1_ready, n - 1)
                for t in range(w):
                    a = act.activation(sq1[:, u % 2, t, :], pY[u % 2][:, E * t:E * (t + 1)], ACT.Square, accum_out=ss1[:, u % 2, t:t + 1])
                a.then_inc(summed1, 1)

            def root1(q, u):
                n = UNITS * q + u
                w = 2 * (CHUNKS[u][1] - CHUNKS[u][0])
                act.wait_ge(summed1, n + 1)
                after(act, rstd1_ready, n - 1)
                act.activation(std1[:, u % 2, 0:w], ss1[:, u % 2, 0:w], ACT.Sqrt, bias=eps[:, :],
                               scale=1.0 / E).then_inc(std1_ready, 1)

            def square2(q, u):
                n = UNITS * q + u
                act.wait_ge(y2_ready, n + 1)
                after(act, summed2, n - 1)
                act.activation(sq2[:, u % 2], y2[:, u % 2], ACT.Square).then_inc(squared2, 1)

            def root2(q, u):
                n = UNITS * q + u
                act.wait_ge(summed2, n + 1)
                after(act, rstd2_ready, n - 1)
                act.activation(std2[:, u % 2], ss2[:, u % 2], ACT.Sqrt, bias=eps[:, :],
                               scale=1.0 / PROJ).then_inc(std2_ready, 1)

            def copy_cross(q, u):
                n = UNITS * q + u
                for h in range(HALVES):
                    act.wait_ge(cross_done, HALVES * n + h + 1)
                    if u % (UNITS // RELAY) == 0 and h == 0:
                        after(act, relaid, RELAY * (q - 1) + u // (UNITS // RELAY) + 2)
                    g = (UB // BLOCK) * u + HB * h
                    act.activation(crossed[:, :, g:g + HB].rearrange("p c g -> p g c"),
                                   pZ[h][:, 0:HB * BW].rearrange("p (g c) -> p g c", c=BW),
                                   ACT.Copy).then_inc(cross_copied, 1)

            def root_link(q):
                act.wait_ge(link_mean, q + 1)
                act.activation(wstd[:, :], wmv[:, 1:2], ACT.Sqrt, bias=eps[:, :]).then_inc(link_std, 1)

            def copy_hz(q):
                act.wait_ge(z_transposed, q + 1)
                act.activation(hz[:, :, :], pW[:, 0:KZ * QB].rearrange("p (k b) -> p k b", b=QB),
                               ACT.Copy).then_inc(hz_ready, 1)

            def relu1(q):
                act.wait_ge(top1_done, q + 1)
                act.wait_ge(pW_free, 1)
                for c in range(K1):
                    a = act.activation(h1[:, c, :], pW[:, QB * c:QB * (c + 1)], ACT.Relu, bias=bias1[:, c:c + 1])
                a.then_inc(h1_ready, 1)

            def relu2(q):
                act.wait_ge(top2_done, q + 1)
                for c in range(K2):
                    a = act.activation(h2[:, c, :], pW[:, QB * c:QB * (c + 1)], ACT.Relu, bias=b2_sb[:, c:c + 1])
                a.then_inc(h2_ready, 1)

            def step(i, s):
                first = isinstance(i, int) and i == 0
                if (at := unit(i, s, LAG_Y)):
                    copy_embT(*at)
                if (at := unit(i, s, LAG_Y2)):
                    square2(*at)
                if (at := unit(i, s, LAG_Z)):
                    copy_cross(*at)
                if (at := unit(i, s, LAG_Y)):
                    square1(*at)
                    root1(*at)
                if first and s == 2:
                    root_x()
                if first and s == 4:
                    make_sx()
                if (at := quarter(i, s, LINKED)):
                    root_link(*at)
                if (at := quarter(i, s, TRANSPOSE)):
                    copy_hz(*at)
                if (at := quarter(i, s, TOP1[-1][0])):
                    relu1(*at)
                if (at := quarter(i, s, TOP2)):
                    relu2(*at)
                if (at := unit(i, s, LAG_Y2)):
                    root2(*at)

            act.wait_ge(consts_ready, 1)
            act.activation(std2[:, 0, 0:1], eps[:, :], ACT.Sqrt)
            run_rounds(act, step)

        @block.vector
        def _(dve):
            V = nc.vector

            def prepare():
                V.memset(ones[:, :], 1.0)
                V.memset(tx[:, :, :, BW - 1:BW], 1.0)
                V.memset(extraT[2 * PROJ:3 * PROJ, :], 1.0).then_inc(relaid, 1)
                V.memset(eps[:, :], EPS).then_inc(consts_ready, 1)
                dve.wait_ge(ids_in, 32)
                V.tensor_tensor(rows_sb[:, :], ids_sb[:, :], bases_sb[:, :], ALU.add).then_inc(rows_ready, 1)
                dve.wait_ge(ws_in, 32)
                V.tensor_reduce(ws_mean[:, :], ws_sb[:, :, :], AX.X, ALU.add).then_inc(ws_steps, 1)
                dve.wait_ge(ws_steps, 1)
                V.tensor_scalar(ws_mean[:, :], ws_mean[:, :], 1.0 / E, None, ALU.mult).then_inc(ws_steps, 1)
                dve.wait_ge(ws_steps, 2)
                V.tensor_tensor(ws_sb[:, :, :], ws_sb[:, :, :], ws_mean[:, :, None].broadcast_to([P, 2, E]),
                                ALU.subtract).then_inc(ws_steps, 1)

            def centre_mix(u):
                first, last = mix_part(u)
                part, mean = mix_sb[:, first:last, :], mix_mean[:, first:last]
                dve.wait_ge(mix_in[u], 16)
                V.tensor_reduce(mean, part, AX.X, ALU.add).then_inc(mix_steps, 1)
                dve.wait_ge(mix_steps, 2 * u + 1)
                V.tensor_scalar(mean, mean, 1.0 / PROJ, None, ALU.mult).then_inc(mix_steps, 1)
                dve.wait_ge(mix_steps, 2 * u + 2)
                V.tensor_tensor(part, part, mean[:, :, None].broadcast_to([P, last - first, PROJ]),
                                ALU.subtract).then_inc(mix_ready, 1)

            def stats_x():
                dve.wait_ge(x_projected, 1)
                for t in range(QUARTERS):
                    V.bn_stats(xstat[:, t, :], pW[:, E * t:E * (t + 1)]).then_inc(x_stats, 1)
                dve.wait_ge(x_stats, QUARTERS)
                for t in range(QUARTERS):
                    V.bn_aggr(xmv[:, t, :], xstat[:, t, :]).then_inc(x_stats, 1)

            def norm_x():
                dve.wait_ge(x_std, 1)
                V.reciprocal(xrstd[:, :], xstd[:, :]).then_inc(x_rstd, 1)
                dve.wait_ge(x_rstd, 1)
                for t in range(QUARTERS):
                    v = V.tensor_scalar(xn[:, t, :], pW[:, E * t:E * (t + 1)], xmv[:, t, 0:1], xrstd[:, t:t + 1],
                                        ALU.subtract, ALU.mult)
                v.then_inc(x_normed, 1)

            def affine_x():
                dve.wait_ge(x_transposed, 1)
                V.tensor_scalar(xT[:, :, :, :].rearrange("e q b g -> e (q b g)"), pZ[1][:, :], gd_sb[:, :],
                                bd_sb[:, :], ALU.mult, ALU.add).then_inc(x_ready, 1)

            def make_shift():
                dve.wait_ge(shift_made, 1)
                dve.wait_ge(gsbs_in, 32)
                V.tensor_copy(shift[:, :], pZ[0][:, 0:PROJ]).then_inc(shift_ready, 1)

            def fold_link():
                dve.wait_ge(wl_in, 16 * (PAIR_TILES // 2 + 6))
                V.tensor_tensor(gg[:, :], gpq_sb[:, 0, :], gpq_sb[:, 1, :], ALU.mult).then_inc(gg_ready, 1)
                V.scalar_tensor_tensor(fold_sb[:, :, XROWS - 1], bpq_sb[:, 0, :], float(E), bpq_sb[:, 1, :],
                                       ALU.mult, ALU.mult).then_inc(fold_ready, 1)

            def scale_link():
                dve.wait_ge(wx_made, 1)
                V.tensor_scalar(wx[:, :], pW[0:XROWS, :], xscale_sb[:, :], None, ALU.mult).then_inc(wx_ready, 1)

            def scale_wl(tiles):
                dve.wait_ge(gg_ready, 1)
                for k in tiles:
                    V.tensor_scalar(wl_sb[:, k, :], wl_sb[:, k, :], gg[:, k:k + 1], None,
                                    ALU.mult).then_inc(wl_ready, 1)

            def scale_top():
                dve.wait_ge(bias1_made, 1)
                dve.wait_ge(top_in, 112)
                V.tensor_tensor(bias1[:, :], pW[:, 0:K1], b1_sb[:, :], ALU.add).then_inc(pW_free, 1)
                for k in range(KZ):
                    V.tensor_scalar(w1_sb[:, k, :], w1_sb[:, k, :], gl_sb[:, k:k + 1], None,
                                    ALU.mult).then_inc(w1_ready, 1)

            def invert1(q, u):
                n = UNITS * q + u
                w = 2 * (CHUNKS[u][1] - CHUNKS[u][0])
                dve.wait_ge(std1_ready, n + 1)
                after(dve, yn_ready, n - 1)
                V.reciprocal(rstd1[:, u % 2, 0:w], std1[:, u % 2, 0:w]).then_inc(rstd1_ready, 1)

            def norm1(q, u):
                n = UNITS * q + u
                lo, hi = 2 * CHUNKS[u][0], 2 * CHUNKS[u][1]
                w = hi - lo
                dve.wait_ge(rstd1_ready, n + 1)
                after(dve, mixed, n - UNITS + 2)
                V.tensor_tensor(yn[:, lo:hi, :], pY[u % 2][:, 0:w * E].rearrange("p (t e) -> p t e", e=E),
                                rstd1[:, u % 2, 0:w, None].broadcast_to([P, w, E]), ALU.mult).then_inc(yn_ready, 1)

            def affine2(q, u):
                n = UNITS * q + u
                dve.wait_ge(mixed, n + 1)
                after(dve, squared2, n - 1)
                after(dve, t_ready, n - 1)
                V.scalar_tensor_tensor(y2[:, u % 2], pA[u % 2][:, :].rearrange("e (b c) -> e b c", c=PROJ),
                                       gs_sb[:, :], shift[:, None, :].broadcast_to([E, UB, PROJ]),
                                       ALU.mult, ALU.add).then_inc(y2_ready, 1)

            def sum2(q, u):
                n = UNITS * q + u
                dve.wait_ge(squared2, n + 1)
                after(dve, std2_ready, n - 1)
                V.tensor_reduce(ss2[:, u % 2], sq2[:, u % 2], AX.X, ALU.add).then_inc(summed2, 1)

            def invert2(q, u):
                n = UNITS * q + u
                dve.wait_ge(std2_ready, n + 1)
                after(dve, t_ready, n - 1)
                V.reciprocal(rstd2[:, u % 2], std2[:, u % 2]).then_inc(rstd2_ready, 1)

            def place_x(q, u):
                n = UNITS * q + u
                after(dve, cross_done, HALVES * (n - 1))
                g = (UB // BLOCK) * u
                V.tensor_copy(tx[:, u % 2, :, BT:BT + BLOCK],
                              xT[:, q, :, g:g + UB // BLOCK].rearrange("e b g -> e g b")
                              if isinstance(q, int) else
                              xT[:, bass.ds(q, 1), :, g:g + UB // BLOCK].rearrange("e o b g -> e (o g) b")
                              ).then_inc(x_placed, 1)

            def norm2(q, u):
                n = UNITS * q + u
                dve.wait_ge(rstd2_ready, n + 1)
                V.tensor_tensor(tx[:, u % 2, :, 0:BT].rearrange("e g (b c) -> e g b c", b=BLOCK),
                                y2[:, u % 2].rearrange("e (g b) c -> e g b c", b=BLOCK),
                                rstd2[:, u % 2].rearrange("e (g b) -> e g b", b=BLOCK)[:, :, :, None]
                                .broadcast_to([E, UB // BLOCK, BLOCK, PROJ]), ALU.mult).then_inc(t_ready, 1)

            def relay(q, part, samples):
                width = GROUPS // RELAY
                groups = slice(width * part, width * (part + 1))
                dve.wait_ge(cross_copied, HALVES * (UNITS * q + UNITS // RELAY * (part + 1)))
                for b4 in samples:
                    rows, at = slice(PROJ * b4, PROJ * (b4 + 1)), GROUPS * b4 + width * part
                    for j in range(QT):
                        V.tensor_copy(pairsT[PROJ * j:PROJ * (j + 1), :, at:at + width],
                                      crossed[rows, PROJ * b4 + j:PROJ * (b4 + 1):QT, groups])
                    V.tensor_copy(extraT[0:PROJ, at:at + width], crossed[rows, BT + b4, groups])
                    last = V.tensor_copy(extraT[PROJ:2 * PROJ, at:at + width], crossed[rows, BW - 1, groups])
                if part == RELAY - 1 and BLOCK - 1 in samples:
                    last = V.tensor_copy(extraT[2 * PROJ:2 * PROJ + 1, :],
                                         sx[0:1, QB * q:QB * (q + 1)] if isinstance(q, int) else sx[0:1, bass.ts(q, QB)])
                if BLOCK - 1 in samples:
                    last.then_inc(relaid, 1)

            def link_norm(q):
                dve.wait_ge(linked, q + 1)
                V.bn_stats(wstat[:, :], pW[:, :]).then_inc(link_stats, 1)
                dve.wait_ge(consts_ready, 1)
                dve.wait_ge(link_stats, q + 1)
                V.bn_aggr(wmv[:, :], wstat[:, :]).then_inc(link_mean, 1)
                dve.wait_ge(link_std, q + 1)
                V.reciprocal(wrstd[:, :], wstd[:, :]).then_inc(link_rstd, 1)
                dve.wait_ge(link_rstd, q + 1)
                V.tensor_scalar(zn[:, :], pW[:, 0:DIMS_IN_USE], wmv[:, 0:1], wrstd[:, :],
                                ALU.subtract, ALU.mult).then_inc(z_ready, 1)

            def copy_y(q):
                dve.wait_ge(top3_done, q + 1)
                y_q = y_all[:, q, :] if isinstance(q, int) else y_all[:, bass.ds(q, 1), :].rearrange("o q b -> o (q b)")
                V.tensor_scalar(y_q, pW[0:1, 0:QB], 1.0, None, ALU.mult).then_inc(pW_free, 1)

            def step(i, s):
                first = isinstance(i, int) and i == 0
                if first and s == 2:
                    stats_x()
                    make_shift()
                if first and s == 3:
                    norm_x()
                if first and s == 4:
                    affine_x()
                if first and s == 6:
                    fold_link()
                if first and s == 7:
                    scale_link()
                if isinstance(i, int) and i == 1 and s == 0:
                    scale_top()
                if isinstance(i, int) and i == 1 and s < PAIR_TILES // 2:
                    scale_wl(range(2 * s, 2 * s + 2))
                if (at := unit(i, s, LAG_Y2)):
                    affine2(*at)
                if (at := unit(i, s, LAG_YN)):
                    invert1(*at)
                    norm1(*at)
                if (at := unit(i, s, LAG_T)):
                    invert2(*at)
                    place_x(*at)
                    norm2(*at)
                if (at := unit(i, s, LAG_Y2)):
                    sum2(*at)
                if first and s < len(MIX) - 1:
                    centre_mix(s + 1)
                for when, part, samples in RELAYS:
                    if (at := quarter(i, s, when)):
                        relay(*at, part, samples)
                if (at := quarter(i, s, LINKED)):
                    link_norm(*at)
                if (at := quarter(i, s, TOP3)):
                    copy_y(*at)

            prepare()
            centre_mix(0)
            run_rounds(dve, step)


def kernel(**inputs):
    import concourse.bacc as bacc
    from concourse.bass_utils import run_bass_kernel_spmd

    a = {name: np.asarray(value) for name, value in inputs.items()}
    tables = [a[f"tbl_{n}"] for n in range(N_SPARSE)]
    f32 = a["W_top1"].dtype

    starts = np.cumsum([0] + [t.shape[0] for t in tables[:-1]]).astype(np.int32)
    bases = np.tile(starts, BATCH).reshape(QUARTERS * TILES, P).T
    ids = a["ids"].reshape(QUARTERS * TILES, P).T

    ws = np.zeros((P, 2, E), f32)
    ws[:D_SPARSE, 0] = ws[D_SPARSE:, 1] = a["L0_rec_Ws"].T

    wmix = np.zeros((P, MIX_COLS // PROJ, PROJ), f32)
    for u, segs in enumerate(MIX):
        for t, first, count, col in segs:
            for b in range(count):
                for n in range(N_SPARSE):
                    r = (UB * u + first + b) * N_SPARSE + n - t * P
                    if 0 <= r < P:
                        wmix[r, col // PROJ + b] = a["L0_rec_Wsi"][:, n]

    dense = a["r_dense_t"].reshape(QUARTERS, GROUPS, BLOCK, KD, P).transpose(4, 3, 0, 2, 1).reshape(P, KD, BATCH)
    wd = a["L0_rec_Wd"].T.reshape(KD, P, E).transpose(1, 0, 2)

    wl = np.zeros((PAIR_TILES * P, MAXD), f32)
    gpq = np.zeros((2, PAIR_TILES * P), f32)
    bpq = np.zeros((2, PAIR_TILES * P), f32)
    fold = np.zeros((PAIR_TILES * P, XROWS), f32)
    g, b = a["L0_rec_gsi"], a["L0_rec_bsi"]
    for r, (p, q) in enumerate(pair_rows()):
        if p > q:
            wl[r] = a["L0_rec_Wl"][:, (p + 1) * p // 2 + q + 1]
            gpq[:, r] = g[p], g[q]
            bpq[:, r] = b[p], b[q]
            fold[r, PROJ + p], fold[r, PROJ + q] = b[q], b[p]
    wlx = a["L0_rec_Wl"][:, [(p + 1) * p // 2 for p in range(PROJ)]].T
    foldx = np.zeros((PROJ, XROWS), f32)
    foldx[np.arange(PROJ), np.arange(PROJ)] = 1
    foldx[:, 2 * PROJ] = b
    xscale = np.concatenate([g, g, np.ones(2, f32)])[:, None]

    def k_tiles(w):
        return w.reshape(-1, P, *w.shape[1:]).swapaxes(0, 1)

    arrays = {
        "tables": np.concatenate(tables), "ids": ids, "bases": bases, "eye": np.eye(P, dtype=f32), "ws": ws,
        "wmix": wmix, "gs": a["L0_rec_gs"][:, None], "bs": a["L0_rec_bs"][None, :], "dense": dense, "wd": wd,
        "gd": a["L0_rec_gd"][:, None], "bd": a["L0_rec_bd"][:, None], "wl": k_tiles(wl), "wlx": wlx,
        "gpq": gpq.reshape(2, PAIR_TILES, P).transpose(2, 0, 1), "bpq": bpq.reshape(2, PAIR_TILES, P).transpose(2, 0, 1),
        "fold": k_tiles(fold), "foldx": foldx, "xscale": xscale,
        "w1": k_tiles(np.concatenate([a["W_top1"][:DIMS_IN_USE], a["W_top1"][MAXD:]])),
        "b1": k_tiles(a["b_top1"]), "w2": k_tiles(a["W_top2"]), "b2": k_tiles(a["b_top2"]),
        "w3": k_tiles(a["W_top3"])[:, :, 0],
        "gl": k_tiles(a["L0_rec_gl"][:DIMS_IN_USE]), "bl": k_tiles(a["L0_rec_bl"][:DIMS_IN_USE]),
    }
    arrays = {f"in_{k}": np.ascontiguousarray(v) for k, v in arrays.items()}

    nc = bacc.Bacc("TRN2", target_bir_lowering=False, num_devices=1)
    args = [nc.dram_tensor(k, v.shape, mybir.dt.from_np(v.dtype), kind="ExternalInput").ap() for k, v in arrays.items()]
    out = nc.dram_tensor("out_y", (1, QUARTERS, QB), mybir.dt.float32, kind="ExternalOutput").ap()
    tower(nc, *args, out)
    r = run_bass_kernel_spmd(nc, [arrays], core_ids=[0])
    y = np.asarray(r.results[0]["out_y"])
    return y.reshape(QUARTERS, BLOCK, GROUPS).transpose(0, 2, 1).reshape(BATCH, 1)
```

```python
from contextlib import ExitStack

import concourse.bass as bass
import numpy as np
from concourse import mybir

P = 128
BATCH, N_SPARSE, D_SPARSE, D_DENSE = 512, 26, 64, 256
E, PROJ, MAXD, DIMS_IN_USE = 128, 32, 512, 384
H1, H2 = 512, 256
EPS = 1e-5

QUARTERS = 4
QB = BATCH // QUARTERS
UNITS = 8
UB = QB // UNITS
TILES = QB * N_SPARSE // P
PERIOD = TILES // 2
BLOCK = P // PROJ
GROUPS = QB // BLOCK
UG = UB // BLOCK
SW = PROJ + 2
KD = D_DENSE // P
KZ = DIMS_IN_USE // P
KTOP = KZ + KD
K1, K2 = H1 // P, H2 // P
XROWS = 2 * PROJ + 2
QT = P // PROJ
COLUMN_TILES = PROJ // QT
PAIR_TILES = COLUMN_TILES // 2
RELAY = 2


def chunk_pairs():
    need = [-(-(UB * N_SPARSE * (u + 1)) // (2 * P)) for u in range(UNITS)]
    return [(a, b) for a, b in zip([0] + need[:-1], need)]


def segments():
    out, col = [], 0
    for u in range(UNITS // 2):
        segs = []
        lo, hi = UB * u, UB * (u + 1)
        for t in range(PERIOD):
            first = max(lo, t * P // N_SPARSE)
            last = min(hi - 1, (t * P + P - 1) // N_SPARSE)
            if first <= last:
                segs.append((t, first - lo, last - first + 1, col))
                col += (last - first + 1) * PROJ
        out.append(segs)
    return out, col


CHUNKS = chunk_pairs()
MIX, MIX_COLS = segments()


def pair_rows():
    out = []
    for kt in range(PAIR_TILES):
        for k in range(P):
            p, q = k % PROJ, QT * kt + k // PROJ
            upper = not q < p <= q + PROJ // 2
            out.append((p, q + PROJ // 2 * upper, upper))
    return out


def tower(nc, tables, ids, bases, eye, ws, wsi, owner, gs, bs, dense, wd, gd, bd, wl, wlx, upper, gpq, bpq, fold,
          foldx, xscale, w1, b1, w2, b2, w3, gl, bl, out):
    f32, i32 = mybir.dt.float32, mybir.dt.int32
    ALU, ACT, AX = mybir.AluOpType, mybir.ActivationFunctionType, mybir.AxisListType

    ctx = ExitStack()
    with ctx:
        def sb(name, shape, dt=f32):
            return ctx.enter_context(nc.sbuf_tensor(name, shape, dt))

        def bank(name):
            return ctx.enter_context(nc.psum_tensor(name, [P, 512], f32))

        def sem(name):
            return ctx.enter_context(nc.semaphore(name))

        ids_sb = sb("ids_sb", [P, QUARTERS * TILES], i32)
        bases_sb = sb("bases_sb", [P, QUARTERS * TILES], i32)
        rows_sb = sb("rows_sb", [P, QUARTERS * TILES], i32)
        eye_sb = sb("eye_sb", [P, P])
        emb = sb("emb", [P, TILES, D_SPARSE])
        embT = sb("embT", [P, 2, 2 * P])
        ws_sb = sb("ws_sb", [P, 2, E])
        ws_mean = sb("ws_mean", [P, 2])
        sq1 = sb("sq1", [P, 2, 4, E])
        ss1 = sb("ss1", [P, 2, 4])
        std1 = sb("std1", [P, 2, 4])
        rstd1 = sb("rstd1", [P, 2, 4])
        yn = sb("yn", [P, TILES, E])
        mix_sb = sb("mix_sb", [P, MIX_COLS // PROJ, PROJ])
        wsi_sb = sb("wsi_sb", [P, PERIOD, PROJ])
        wsi_mean = sb("wsi_mean", [P, PERIOD])
        owner_sb = sb("owner_sb", [P, MIX_COLS // PROJ])
        gs_sb = sb("gs_sb", [E, 1])
        bs_rep = sb("bs_rep", [N_SPARSE, E])
        shift = sb("shift", [E, PROJ])
        y2 = sb("y2", [E, 2, UB, PROJ])
        sq2 = sb("sq2", [E, 2, UB, PROJ])
        ss2 = sb("ss2", [E, 2, UB])
        std2 = sb("std2", [E, 2, UB])
        rstd2 = sb("rstd2", [E, 2, UB])
        tx = sb("tx", [E, 2, UB, SW])
        crossed = sb("crossed", [P, SW, GROUPS])
        pairsT = sb("pairsT", [P, COLUMN_TILES, QB])
        extraT = sb("extraT", [P, QB])
        dense_sb = sb("dense_sb", [P, KD, BATCH])
        wd_sb = sb("wd_sb", [P, KD, E])
        gd_sb = sb("gd_sb", [E, 1])
        bd_sb = sb("bd_sb", [E, 1])
        xstat = sb("xstat", [P, QUARTERS, 6])
        xmv = sb("xmv", [P, QUARTERS, 2])
        xstd = sb("xstd", [P, QUARTERS])
        xrstd = sb("xrstd", [P, QUARTERS])
        xn = sb("xn", [P, QUARTERS, E])
        xT = sb("xT", [E, QUARTERS, BLOCK, GROUPS])
        sx = sb("sx", [1, BATCH])
        ones = sb("ones", [P, 1])
        zeros = sb("zeros", [P, 512])
        eps = sb("eps", [P, 1])
        wl_sb = sb("wl_sb", [P, PAIR_TILES, MAXD])
        wlx_sb = sb("wlx_sb", [PROJ, MAXD])
        wx = sb("wx", [XROWS, MAXD])
        upper_sb = sb("upper_sb", [P, PAIR_TILES], i32)
        gpq_sb = sb("gpq_sb", [P, 2, PAIR_TILES])
        bpq_sb = sb("bpq_sb", [P, 2, PAIR_TILES])
        gg = sb("gg", [P, PAIR_TILES])
        fold_sb = sb("fold_sb", [P, PAIR_TILES, XROWS])
        foldx_sb = sb("foldx_sb", [PROJ, XROWS])
        xscale_sb = sb("xscale_sb", [XROWS, 1])
        w1_sb = sb("w1_sb", [P, KTOP, H1])
        b1_sb = sb("b1_sb", [P, K1])
        w2_sb = sb("w2_sb", [P, K1, H2])
        b2_sb = sb("b2_sb", [P, K2])
        w3_sb = sb("w3_sb", [P, K2])
        gl_sb = sb("gl_sb", [P, KZ])
        bl_sb = sb("bl_sb", [P, KZ])
        wstat = sb("wstat", [P, 6])
        wmv = sb("wmv", [P, 2])
        wstd = sb("wstd", [P, 1])
        wrstd = sb("wrstd", [P, 1])
        zn = sb("zn", [P, DIMS_IN_USE])
        hz = sb("hz", [P, KZ, QB])
        h1 = sb("h1", [P, K1, QB])
        h2 = sb("h2", [P, K2, QB])
        y_all = sb("y_all", [1, QUARTERS, QB])

        pT = bank("pT")
        pY = [bank("pY0"), bank("pY1")]
        pA = [bank("pA0"), bank("pA1")]
        pZ = bank("pZ")
        pL = bank("pL")
        pW = bank("pW")

        ids_in = sem("ids_in")
        ws_in = sem("ws_in")
        dense_in = sem("dense_in")
        wsi_in = sem("wsi_in")
        gsbs_in = sem("gsbs_in")
        gdbd_in = sem("gdbd_in")
        fold_in = sem("fold_in")
        wl_in = [sem(f"wl_in{k}") for k in range(PAIR_TILES)]
        wlx_in = sem("wlx_in")
        upper_in = sem("upper_in")
        top_in = sem("top_in")
        rows_ready = sem("rows_ready")
        zeros_ready = sem("zeros_ready")
        consts_ready = sem("consts_ready")
        ws_steps = sem("ws_steps")
        wsi_steps = sem("wsi_steps")
        mix_ready = sem("mix_ready")
        x_projected = sem("x_projected")
        x_stats = sem("x_stats")
        x_std = sem("x_std")
        x_rstd = sem("x_rstd")
        x_normed = sem("x_normed")
        x_transposed = sem("x_transposed")
        x_ready = sem("x_ready")
        shift_made = sem("shift_made")
        shift_ready = sem("shift_ready")
        sx_made = sem("sx_made")
        sx_ready = sem("sx_ready")
        gg_ready = sem("gg_ready")
        fold_ready = sem("fold_ready")
        wx_made = sem("wx_made")
        wl_ready = sem("wl_ready")
        gathered = [sem(f"gathered{u}") for u in range(UNITS)]
        transposed = sem("transposed")
        embT_ready = sem("embT_ready")
        projected = sem("projected")
        summed1 = sem("summed1")
        std1_ready = sem("std1_ready")
        rstd1_ready = sem("rstd1_ready")
        yn_ready = sem("yn_ready")
        mixed = sem("mixed")
        y2_ready = sem("y2_ready")
        squared2 = sem("squared2")
        summed2 = sem("summed2")
        std2_ready = sem("std2_ready")
        rstd2_ready = sem("rstd2_ready")
        x_placed = sem("x_placed")
        t_ready = sem("t_ready")
        cross_done = sem("cross_done")
        cross_copied = sem("cross_copied")
        relaid = [sem(f"relaid{part}") for part in range(RELAY)]
        relaid_act = [sem(f"relaid_act{part}") for part in range(RELAY)]
        extra_ready = sem("extra_ready")
        overlaid = sem("overlaid")
        linked = sem("linked")
        link_stats = sem("link_stats")
        link_mean = sem("link_mean")
        link_std = sem("link_std")
        link_rstd = sem("link_rstd")
        z_ready = sem("z_ready")
        z_transposed = sem("z_transposed")
        hz_ready = sem("hz_ready")
        top1_done = sem("top1_done")
        h1_ready = sem("h1_ready")
        top2_done = sem("top2_done")
        h2_ready = sem("h2_ready")
        hz_by_dve = sem("hz_by_dve")
        h1_by_dve = sem("h1_by_dve")
        h2_by_dve = sem("h2_by_dve")
        top3_done = sem("top3_done")
        pW_free = sem("pW_free")
        y_out = sem("y_out")

        def after(eng, semaphore, value):
            if not (isinstance(value, int) and value <= 0):
                eng.wait_ge(semaphore, value)

        def run_rounds(eng, step):
            for i in (0, 1):
                for s in range(UNITS):
                    step(i, s)
            with eng.Fori(2, QUARTERS) as i:
                for s in range(UNITS):
                    step(i, s)
            for s in range(LAG_Z):
                step(QUARTERS, s)

        def unit(i, s, lag):
            q, u = (i, s - lag) if s >= lag else (i - 1, s - lag + UNITS)
            if isinstance(i, int) and (q < 0 or q >= QUARTERS):
                return None
            return q, u

        def quarter(i, s, when):
            if s != when[1] or isinstance(i, int) and not 0 <= i - when[0] < QUARTERS:
                return None
            if isinstance(i, int) and i == QUARTERS and when > LAST_STEP:
                return None
            return (i - when[0],)

        TOP_LOADS = 16 * (KTOP + 6)

        LAG_Y, LAG_YN, LAG_A, LAG_Y2, LAG_T, LAG_Z = 1, 2, 2, 3, 4, 5
        DVE_RELAYS = [((1, 2), 0, (0,)), ((1, 3), 0, (1,)), ((1, 4), 0, (2,)), ((1, 5), 1, (0,)), ((1, 6), 1, (1,))]
        ACT_RELAYS = [((1, 3), 0, (3,)), ((1, 5), 1, (3,)), ((1, 6), 1, (2,))]
        OVERLAY = (1, 7)
        LINKS = [((1, 7), 0, 1), ((2, 0), 1, 2), ((2, 1), 2, PAIR_TILES)]
        LINKED = LINKS[-1][0]
        TRANSPOSE = (2, 2)
        TOP1_DENSE = [((2, 1), 0, 1), ((2, 2), 1, K1)]
        TOP1 = [((2, 3), 0, 2), ((2, 4), 2, K1)]
        TOP2 = (2, 5)
        TOP3 = (2, 6)
        LAST_STEP = (2, 2)
        FOLDS = [(0, 1), (1, 2), (2, 3), (3, PAIR_TILES)]
        WARM_START = 4
        LAST = QUARTERS - 1
        TOP1_BANKS, TOP2_BANKS = [*pY, *pA], [pZ, pT]
        HZ_ON_ACT = 1

        def is_last(q):
            return isinstance(q, int) and q == LAST

        def top1_out(q, c):
            return TOP1_BANKS[c][:, 0:QB] if is_last(q) else pW[:, QB * c:QB * (c + 1)]

        def hz_bank(q, k):
            return pZ if is_last(q) and k < HZ_ON_ACT else pL

        def calls(relays, part):
            return len([r for r in relays if r[1] == part])

        block = ctx.enter_context(nc.Block())

        def relay(copy, part, samples):
            width = GROUPS // RELAY
            groups = slice(width * part, width * (part + 1))
            for b4 in samples:
                rows, at = slice(PROJ * b4, PROJ * (b4 + 1)), GROUPS * b4 + width * part
                for j in range(QT):
                    copy(pairsT[PROJ * j:PROJ * (j + 1), :, at:at + width],
                         crossed[rows, j:PROJ:QT, groups])
                copy(extraT[0:PROJ, at:at + width], crossed[rows, PROJ, groups])
                last = copy(extraT[PROJ:2 * PROJ, at:at + width], crossed[rows, PROJ + 1, groups])
            return last

        @block.gpsimd
        def _(pool):
            pool.wait_ge(rows_ready, 1)
            for q in range(QUARTERS):
                for u in range(UNITS):
                    lo, hi = 2 * CHUNKS[u][0], 2 * CHUNKS[u][1]
                    after(pool, transposed, UNITS * (q - 1) + u + 1)
                    for t in range(lo, hi):
                        c = q * TILES + t
                        nc.gpsimd.indirect_dma_start(
                            emb[:, t, :], None, tables[:, :],
                            bass.IndirectOffsetOnAxis(rows_sb[:, c:c + 1], 0)).then_inc(gathered[u], 16)

        @block.sync
        def _(sp):
            sp.dma_start(ids_sb[:, :], ids).then_inc(ids_in, 16)
            sp.dma_start(bases_sb[:, :], bases).then_inc(ids_in, 16)
            sp.dma_start(dense_sb[:, :, :], dense).then_inc(dense_in, 16)
            sp.dma_start(wd_sb[:, :, :], wd).then_inc(dense_in, 16)
            sp.dma_start(ws_sb[:, :, :], ws).then_inc(ws_in, 16)
            sp.dma_start(eye_sb[:, :], eye).then_inc(ws_in, 16)
            sp.dma_start(wsi_sb[:, :, :], wsi).then_inc(wsi_in, 16)
            sp.dma_start(owner_sb[:, :], owner).then_inc(wsi_in, 16)
            sp.dma_start(gs_sb[:, :], gs).then_inc(gsbs_in, 16)
            sp.dma_start(bs_rep[:, :], bs.broadcast_to([N_SPARSE, E])).then_inc(gsbs_in, 16)
            sp.dma_start(gd_sb[:, :], gd).then_inc(gdbd_in, 16)
            sp.dma_start(bd_sb[:, :], bd).then_inc(gdbd_in, 16)
            sp.dma_start(gpq_sb[:, :, :], gpq).then_inc(fold_in, 16)
            sp.dma_start(bpq_sb[:, :, :], bpq).then_inc(fold_in, 16)
            sp.dma_start(foldx_sb[:, :], foldx).then_inc(fold_in, 16)
            sp.dma_start(xscale_sb[:, :], xscale).then_inc(fold_in, 16)
            sp.wait_ge(gathered[0], 16 * 4)
            sp.dma_start(fold_sb[:, :, :], fold).then_inc(fold_in, 16)
            for k in range(PAIR_TILES):
                if k == PAIR_TILES - 1:
                    sp.wait_ge(gathered[1], 16 * 4)
                sp.dma_start(wl_sb[:, k, :], wl[:, k, :]).then_inc(wl_in[k], 16)
            sp.dma_start(wlx_sb[:, :], wlx).then_inc(wlx_in, 16)
            sp.dma_start(upper_sb[:, :], upper).then_inc(upper_in, 16)
            sp.wait_ge(gathered[3], 16 * 4)
            sp.dma_start(b1_sb[:, :], b1).then_inc(top_in, 16)
            sp.dma_start(gl_sb[:, :], gl).then_inc(top_in, 16)
            sp.dma_start(bl_sb[:, :], bl).then_inc(top_in, 16)
            for k in range(KTOP):
                sp.dma_start(w1_sb[:, k, :], w1[:, k, :]).then_inc(top_in, 16)
                if k == 2:
                    sp.wait_ge(gathered[4], 16 * 4)
            sp.wait_ge(gathered[5], 16 * 2)
            sp.dma_start(w2_sb[:, :, :], w2).then_inc(top_in, 16)
            sp.dma_start(b2_sb[:, :], b2).then_inc(top_in, 16)
            sp.dma_start(w3_sb[:, :], w3).then_inc(top_in, 16)
            sp.wait_ge(pW_free, QUARTERS + 1)
            sp.dma_start(out, y_all[:, :, :]).then_inc(y_out, 16)
            sp.wait_ge(y_out, 16)

        @block.tensor
        def _(pe):
            def keep_warm(products):
                for _ in range(products):
                    nc.tensor.matmul(pT[:, :], zeros[:, 0:P], zeros[:, :], start=True, stop=True)

            def project_x():
                pe.wait_ge(dense_in, 32)
                for t in range(QUARTERS):
                    for k in range(KD):
                        mm = nc.tensor.matmul(pW[:, E * t:E * (t + 1)], dense_sb[:, k, P * t:P * (t + 1)],
                                              wd_sb[:, k, :], start=k == 0, stop=k == KD - 1)
                mm.then_inc(x_projected, 1)

            def prepare_shift():
                pe.wait_ge(wsi_steps, 3)
                pe.wait_ge(gsbs_in, 32)
                nc.tensor.matmul(pZ[:, 0:PROJ], bs_rep[:, :], wsi_sb[0:N_SPARSE, 0, :],
                                 start=True, stop=True).then_inc(shift_made, 1)

            def transpose_x():
                pe.wait_ge(x_normed, 1)
                for t in range(QUARTERS):
                    mm = nc.tensor.transpose(pL[:, P * t:P * (t + 1)], xn[:, t, :], eye_sb[:, :])
                mm.then_inc(x_transposed, 1)

            def sum_x():
                pe.wait_ge(shift_ready, 1)
                pe.wait_ge(x_ready, 1)
                nc.tensor.matmul(pZ[0:1, :], ones[:, :], xT[:, :, :, :].rearrange("e q b g -> e (q b g)"),
                                 start=True, stop=True).then_inc(sx_made, 1)

            def prepare_link(lo, hi):
                pe.wait_ge(fold_ready, 1)
                for k in range(lo, hi):
                    pe.wait_ge(wl_in[k], 16)
                    nc.tensor.matmul(pW[0:XROWS, :], fold_sb[:, k, :], wl_sb[:, k, :], start=k == 0, stop=False)
                if hi == PAIR_TILES:
                    pe.wait_ge(wlx_in, 16)
                    nc.tensor.matmul(pW[0:XROWS, :], foldx_sb[:, :], wlx_sb[:, :],
                                     start=False, stop=True).then_inc(wx_made, 1)

            def stage_t(q, u):
                n = UNITS * q + u
                lo, hi = CHUNKS[u]
                pe.wait_ge(gathered[u], 32 * (hi - lo) * (q + 1))
                after(pe, embT_ready, n)
                for j in range(lo, hi):
                    mm = nc.tensor.transpose(pT[:, P * (j - lo):P * (j - lo + 1)],
                                             emb[:, 2 * j:2 * j + 2, :].rearrange("p t d -> p (t d)"), eye_sb[:, :])
                mm.then_inc(transposed, 1)

            def stage_y(q, u):
                n = UNITS * q + u
                lo, hi = CHUNKS[u]
                pe.wait_ge(embT_ready, n + 1)
                after(pe, yn_ready, n - 1)
                for j in range(hi - lo):
                    mm = nc.tensor.matmul(pY[u % 2][:, 2 * E * j:2 * E * (j + 1)], embT[:, u % 2, P * j:P * (j + 1)],
                                          ws_sb[:, :, :].rearrange("p t e -> p (t e)"), start=True, stop=True)
                mm.then_inc(projected, 1)

            def stage_a(q, u):
                n = UNITS * q + u
                pe.wait_ge(yn_ready, n + 1)
                if isinstance(q, int) and q == 0 and u < len(MIX):
                    pe.wait_ge(mix_ready, u + 1)
                after(pe, y2_ready, n - 1)
                segs = MIX[u % len(MIX)]
                for t, first, count, col in segs:
                    tile = PERIOD * (u // len(MIX)) + t
                    mm = nc.tensor.matmul(
                        pA[u % 2][:, PROJ * first:PROJ * (first + count)], yn[:, tile, :],
                        mix_sb[:, col // PROJ:col // PROJ + count, :].rearrange("p b c -> p (b c)"),
                        start=t == segs[0][0], stop=t == segs[-1][0], skip_group_check=True)
                mm.then_inc(mixed, 1)

            def stage_z(q, u):
                n = UNITS * q + u
                pe.wait_ge(t_ready, n + 1)
                pe.wait_ge(x_placed, n + 1)
                if isinstance(q, int) and n == 0:
                    pe.wait_ge(sx_ready, 1)
                after(pe, cross_copied, n)
                for b in range(UB):
                    rows = slice(PROJ * (b % BLOCK), PROJ * (b % BLOCK + 1))
                    mm = nc.tensor.matmul(pZ[rows, SW * (b // BLOCK):SW * (b // BLOCK + 1)],
                                          tx[:, u % 2, b, 0:PROJ], tx[:, u % 2, b, :], start=True, stop=True)
                mm.then_inc(cross_done, 1)

            def link(q, lo, hi):
                if lo == 0:
                    after(pe, hz_ready, q)
                    pe.wait_ge(extra_ready, q + 1)
                    if isinstance(q, int) and q == 0:
                        pe.wait_ge(pW_free, 1)
                        pe.wait_ge(wl_ready, PAIR_TILES)
                    nc.tensor.matmul(pL[:, :], extraT[0:XROWS, :], wx[:, :], start=True, stop=False)
                    pe.wait_ge(overlaid, q + 1)
                for k in range(lo, hi):
                    mm = nc.tensor.matmul(pL[:, :], pairsT[:, k, :], wl_sb[:, k, :], start=False,
                                          stop=k == PAIR_TILES - 1)
                if hi == PAIR_TILES:
                    mm.then_inc(linked, 1)

            def transpose_z(q):
                pe.wait_ge(z_ready, q + 1)
                for k in range(KZ):
                    part = slice(P * k, P * (k + 1))
                    mm = nc.tensor.transpose(hz_bank(q, k)[:, part], zn[:, part], eye_sb[:, :])
                mm.then_inc(z_transposed, 1)

            def top1_dense(q, lo, hi):
                pe.wait_ge(top_in, TOP_LOADS)
                if not is_last(q):
                    pe.wait_ge(pW_free, q + 1)
                for c in range(lo, hi):
                    for k in range(KZ, KTOP):
                        nc.tensor.matmul(top1_out(q, c), w1_sb[:, k, P * c:P * (c + 1)],
                                         dense_sb[:, k - KZ, bass.ts(q, QB)],
                                         start=k == KZ and (c == 0 or is_last(q)), stop=False,
                                         skip_group_check=True)

            def top1(q, lo, hi):
                pe.wait_ge(hz_ready, q + 1)
                for c in range(lo, hi):
                    for k in range(KZ):
                        mm = nc.tensor.matmul(top1_out(q, c), w1_sb[:, k, P * c:P * (c + 1)], hz[:, k, :],
                                              start=False, stop=k == KZ - 1 and (c == K1 - 1 or is_last(q)),
                                              skip_group_check=True)
                if hi == K1:
                    mm.then_inc(top1_done, 1)

            def top2(q):
                pe.wait_ge(h1_ready, q + 1)
                for c in range(K2):
                    for k in range(K1):
                        mm = nc.tensor.matmul(pW[:, QB * c:QB * (c + 1)], w2_sb[:, k, P * c:P * (c + 1)], h1[:, k, :],
                                              start=k == 0, stop=k == K1 - 1)
                mm.then_inc(top2_done, 1)

            def top3(q):
                pe.wait_ge(h2_ready, q + 1)
                for k in range(K2):
                    mm = nc.tensor.matmul(pW[0:1, 0:QB], w3_sb[:, k:k + 1], h2[:, k, :],
                                          start=k == 0, stop=k == K2 - 1)
                mm.then_inc(top3_done, 1)

            def step(i, s):
                first = isinstance(i, int) and i == 0
                if isinstance(i, int) and i == QUARTERS and (i - 2, s) > LAST_STEP:
                    keep_warm(1)
                if (at := unit(i, s, LAG_Z)):
                    stage_z(*at)
                if not first and (at := unit(i, s, 0)):
                    stage_t(*at)
                if (at := unit(i, s, LAG_Y)):
                    stage_y(*at)
                if first and (at := unit(i, s, LAG_A)):
                    stage_a(*at)
                for when, lo, hi in LINKS:
                    if (at := quarter(i, s, when)):
                        link(*at, lo, hi)
                for when, lo, hi in TOP1_DENSE:
                    if (at := quarter(i, s, when)):
                        top1_dense(*at, lo, hi)
                if (at := quarter(i, s, TRANSPOSE)):
                    transpose_z(*at)
                for when, lo, hi in TOP1:
                    if (at := quarter(i, s, when)):
                        top1(*at, lo, hi)
                if (at := quarter(i, s, TOP2)):
                    top2(*at)
                if (at := quarter(i, s, TOP3)):
                    top3(*at)
                if first and s == 0:
                    prepare_shift()
                if first and s == 1:
                    keep_warm(2)
                    transpose_x()
                if first and s == 2:
                    sum_x()
                if first and 1 <= s < 1 + len(FOLDS):
                    prepare_link(*FOLDS[s - 1])
                if not first and (at := unit(i, s, LAG_A)):
                    stage_a(*at)
                if first:
                    stage_t(i, s)

            def finish():
                for when, lo, hi in TOP1:
                    if when > LAST_STEP:
                        top1(LAST - 1, lo, hi)
                link(LAST, 0, PAIR_TILES)
                top1_dense(LAST, 0, K1)
                transpose_z(LAST)
                top2(LAST - 1)
                for k in range(KZ):
                    if k < HZ_ON_ACT:
                        pe.wait_ge(hz_ready, LAST + k + 1)
                    else:
                        pe.wait_ge(hz_by_dve, k - HZ_ON_ACT + 1)
                    for c in range(K1):
                        mm = nc.tensor.matmul(TOP1_BANKS[c][:, 0:QB], w1_sb[:, k, P * c:P * (c + 1)], hz[:, k, :],
                                              start=False, stop=k == KZ - 1, skip_group_check=True)
                        if k == KZ - 1:
                            mm.then_inc(top1_done, 1)
                top3(LAST - 1)
                for k in range(K1):
                    if k % 2 == 0:
                        pe.wait_ge(h1_ready, LAST + k // 2 + 1)
                    else:
                        pe.wait_ge(h1_by_dve, k // 2 + 1)
                    for c in range(K2):
                        mm = nc.tensor.matmul(TOP2_BANKS[c][:, 0:QB], w2_sb[:, k, P * c:P * (c + 1)], h1[:, k, :],
                                              start=k == 0, stop=k == K1 - 1)
                        if k == K1 - 1:
                            mm.then_inc(top2_done, 1)
                pe.wait_ge(pW_free, LAST + 1)
                for k in range(K2):
                    if k % 2 == 0:
                        pe.wait_ge(h2_ready, LAST + k // 2 + 1)
                    else:
                        pe.wait_ge(h2_by_dve, k // 2 + 1)
                    mm = nc.tensor.matmul(pW[0:1, 0:QB], w3_sb[:, k:k + 1], h2[:, k, :],
                                          start=k == 0, stop=k == K2 - 1)
                mm.then_inc(top3_done, 1)

            pe.wait_ge(zeros_ready, 1)
            keep_warm(WARM_START)
            project_x()
            pe.wait_ge(ws_in, 32)
            pe.wait_ge(ws_steps, 3)
            run_rounds(pe, step)
            finish()

        @block.scalar
        def _(act):
            def root_x():
                act.wait_ge(x_stats, 2 * QUARTERS)
                act.activation(xstd[:, :], xmv[:, :, 1], ACT.Sqrt, bias=eps[:, :]).then_inc(x_std, 1)

            def make_sx():
                act.wait_ge(sx_made, 1)
                act.activation(sx[:, :], pZ[0:1, :], ACT.Copy).then_inc(sx_ready, 1)

            def scale_wl(k):
                act.wait_ge(gg_ready, 1)
                act.wait_ge(wx_made, 1)
                act.activation(wl_sb[:, k, :], wl_sb[:, k, :], ACT.Copy, scale=gg[:, k:k + 1]).then_inc(wl_ready, 1)

            def copy_embT(q, u):
                n = UNITS * q + u
                w = P * (CHUNKS[u][1] - CHUNKS[u][0])
                act.wait_ge(transposed, n + 1)
                after(act, projected, n - 1)
                act.activation(embT[:, u % 2, 0:w], pT[:, 0:w], ACT.Copy).then_inc(embT_ready, 1)

            def square1(q, u):
                n = UNITS * q + u
                w = 2 * (CHUNKS[u][1] - CHUNKS[u][0])
                act.wait_ge(projected, n + 1)
                after(act, std1_ready, n - 1)
                for t in range(w):
                    a = act.activation(sq1[:, u % 2, t, :], pY[u % 2][:, E * t:E * (t + 1)], ACT.Square,
                                       accum_out=ss1[:, u % 2, t:t + 1])
                a.then_inc(summed1, 1)

            def root1(q, u):
                n = UNITS * q + u
                w = 2 * (CHUNKS[u][1] - CHUNKS[u][0])
                act.wait_ge(summed1, n + 1)
                after(act, rstd1_ready, n - 1)
                act.activation(std1[:, u % 2, 0:w], ss1[:, u % 2, 0:w], ACT.Sqrt, bias=eps[:, :],
                               scale=1.0 / E).then_inc(std1_ready, 1)

            def square2(q, u):
                n = UNITS * q + u
                act.wait_ge(y2_ready, n + 1)
                after(act, summed2, n - 1)
                act.activation(sq2[:, u % 2], y2[:, u % 2], ACT.Square).then_inc(squared2, 1)

            def root2(q, u):
                n = UNITS * q + u
                act.wait_ge(summed2, n + 1)
                after(act, rstd2_ready, n - 1)
                act.activation(std2[:, u % 2], ss2[:, u % 2], ACT.Sqrt, bias=eps[:, :],
                               scale=1.0 / PROJ).then_inc(std2_ready, 1)

            def copy_cross(q, u):
                n = UNITS * q + u
                act.wait_ge(cross_done, n + 1)
                if u % (UNITS // RELAY) == 0:
                    part = u // (UNITS // RELAY)
                    after(act, relaid[part], calls(DVE_RELAYS, part) * q)
                    after(act, relaid_act[part], calls(ACT_RELAYS, part) * q)
                act.activation(crossed[:, :, UG * u:UG * (u + 1)].rearrange("p c g -> p g c"),
                               pZ[:, 0:UG * SW].rearrange("p (g c) -> p g c", c=SW),
                               ACT.Copy).then_inc(cross_copied, 1)

            def root_link(q):
                act.wait_ge(link_mean, q + 1)
                act.activation(wstd[:, :], wmv[:, 1:2], ACT.Sqrt, bias=eps[:, :]).then_inc(link_std, 1)

            def copy_hz(q):
                act.wait_ge(z_transposed, q + 1)
                act.wait_ge(top_in, TOP_LOADS)
                for k in range(KZ):
                    a = act.activation(hz[:, k, :], pL[:, QB * k:QB * (k + 1)], ACT.Identity, bias=bl_sb[:, k:k + 1],
                                       scale=gl_sb[:, k:k + 1])
                a.then_inc(hz_ready, 1)

            def relu1(q):
                act.wait_ge(top1_done, q + 1)
                for c in range(K1):
                    a = act.activation(h1[:, c, :], pW[:, QB * c:QB * (c + 1)], ACT.Relu, bias=b1_sb[:, c:c + 1])
                a.then_inc(h1_ready, 1)

            def relu2(q):
                act.wait_ge(top2_done, q + 1)
                for c in range(K2):
                    a = act.activation(h2[:, c, :], pW[:, QB * c:QB * (c + 1)], ACT.Relu, bias=b2_sb[:, c:c + 1])
                a.then_inc(h2_ready, 1)

            def step(i, s):
                first = isinstance(i, int) and i == 0
                if (first or s == 0 and isinstance(i, int) and i == 1) and (at := unit(i, s, LAG_Y)):
                    copy_embT(*at)
                if first and s == 1:
                    root_x()
                if (at := unit(i, s, LAG_Y2)):
                    square2(*at)
                if (at := unit(i, s, LAG_Z)):
                    copy_cross(*at)
                if not first and (at := unit(i, s, 0)):
                    copy_embT(*at)
                if (at := unit(i, s, LAG_Y)):
                    square1(*at)
                    root1(*at)
                if first and s == 4:
                    make_sx()
                if isinstance(i, int) and i == 1 and s < PAIR_TILES:
                    scale_wl(s)
                for when, part, samples in ACT_RELAYS:
                    if (at := quarter(i, s, when)):
                        relay_on_act(*at, part, samples)
                if (at := quarter(i, s, TOP1[-1][0])):
                    relu1(*at)
                if (at := quarter(i, s, TOP2)):
                    relu2(*at)
                if (at := unit(i, s, LAG_Y2)):
                    root2(*at)
                if (at := quarter(i, s, TRANSPOSE)):
                    copy_hz(*at)
                if (at := quarter(i, s, LINKED)):
                    root_link(*at)

            def relay_on_act(q, part, samples):
                act.wait_ge(cross_copied, UNITS * q + UNITS // RELAY * (part + 1))
                relay(lambda to, of: act.activation(to, of, ACT.Copy), part, samples).then_inc(relaid_act[part], 1)

            def finish():
                for when, part, samples in ACT_RELAYS:
                    if when >= (1, LAG_Z):
                        relay_on_act(LAST, part, samples)
                relu1(LAST - 1)
                root_link(LAST)
                act.wait_ge(z_transposed, LAST + 1)
                for k in range(HZ_ON_ACT):
                    act.activation(hz[:, k, :], hz_bank(LAST, k)[:, QB * k:QB * (k + 1)], ACT.Identity,
                                   bias=bl_sb[:, k:k + 1], scale=gl_sb[:, k:k + 1]).then_inc(hz_ready, 1)
                relu2(LAST - 1)
                for c in range(0, K1, 2):
                    act.wait_ge(top1_done, LAST + c + 1)
                    act.activation(h1[:, c, :], TOP1_BANKS[c][:, 0:QB], ACT.Relu,
                                   bias=b1_sb[:, c:c + 1]).then_inc(h1_ready, 1)
                for c in range(0, K2, 2):
                    act.wait_ge(top2_done, LAST + c + 1)
                    act.activation(h2[:, c, :], TOP2_BANKS[c][:, 0:QB], ACT.Relu,
                                   bias=b2_sb[:, c:c + 1]).then_inc(h2_ready, 1)

            act.wait_ge(consts_ready, 1)
            act.activation(std2[:, 0, 0:1], eps[:, :], ACT.Sqrt)
            run_rounds(act, step)
            finish()

        @block.vector
        def _(dve):
            V = nc.vector

            def prepare():
                V.memset(zeros[:, :], 0.0).then_inc(zeros_ready, 1)
                V.memset(ones[:, :], 1.0)
                V.memset(tx[:, :, :, SW - 1:SW], 1.0)
                V.memset(extraT[2 * PROJ:3 * PROJ, :], 1.0)
                V.memset(eps[:, :], EPS).then_inc(consts_ready, 1)
                dve.wait_ge(ids_in, 32)
                V.tensor_tensor(rows_sb[:, :], ids_sb[:, :], bases_sb[:, :], ALU.add).then_inc(rows_ready, 1)
                dve.wait_ge(ws_in, 32)
                V.tensor_reduce(ws_mean[:, :], ws_sb[:, :, :], AX.X, ALU.add).then_inc(ws_steps, 1)
                dve.wait_ge(ws_steps, 1)
                V.tensor_scalar(ws_mean[:, :], ws_mean[:, :], 1.0 / E, None, ALU.mult).then_inc(ws_steps, 1)
                dve.wait_ge(ws_steps, 2)
                V.tensor_tensor(ws_sb[:, :, :], ws_sb[:, :, :], ws_mean[:, :, None].broadcast_to([P, 2, E]),
                                ALU.subtract).then_inc(ws_steps, 1)

            def centre_wsi():
                dve.wait_ge(wsi_in, 32)
                V.tensor_reduce(wsi_mean[:, :], wsi_sb[:, :, :], AX.X, ALU.add).then_inc(wsi_steps, 1)
                dve.wait_ge(wsi_steps, 1)
                V.tensor_scalar(wsi_mean[:, :], wsi_mean[:, :], 1.0 / PROJ, None, ALU.mult).then_inc(wsi_steps, 1)
                dve.wait_ge(wsi_steps, 2)
                V.tensor_tensor(wsi_sb[:, :, :], wsi_sb[:, :, :],
                                wsi_mean[:, :, None].broadcast_to([P, PERIOD, PROJ]), ALU.subtract).then_inc(wsi_steps, 1)

            def spread_mix(u):
                dve.wait_ge(wsi_steps, 3)
                for t, first, count, col in MIX[u]:
                    blocks = slice(col // PROJ, col // PROJ + count)
                    v = V.tensor_tensor(mix_sb[:, blocks, :], wsi_sb[:, t:t + 1, :].broadcast_to([P, count, PROJ]),
                                        owner_sb[:, blocks, None].broadcast_to([P, count, PROJ]), ALU.mult)
                v.then_inc(mix_ready, 1)

            def stats_x():
                dve.wait_ge(x_projected, 1)
                for t in range(QUARTERS):
                    V.bn_stats(xstat[:, t, :], pW[:, E * t:E * (t + 1)]).then_inc(x_stats, 1)
                dve.wait_ge(x_stats, QUARTERS)
                for t in range(QUARTERS):
                    V.bn_aggr(xmv[:, t, :], xstat[:, t, :]).then_inc(x_stats, 1)

            def norm_x():
                dve.wait_ge(x_std, 1)
                V.reciprocal(xrstd[:, :], xstd[:, :]).then_inc(x_rstd, 1)
                dve.wait_ge(x_rstd, 1)
                for t in range(QUARTERS):
                    v = V.tensor_scalar(xn[:, t, :], pW[:, E * t:E * (t + 1)], xmv[:, t, 0:1], xrstd[:, t:t + 1],
                                        ALU.subtract, ALU.mult)
                v.then_inc(x_normed, 1)

            def affine_x():
                dve.wait_ge(gdbd_in, 32)
                dve.wait_ge(x_transposed, 1)
                V.tensor_scalar(xT[:, :, :, :].rearrange("e q b g -> e (q b g)"), pL[:, :], gd_sb[:, :],
                                bd_sb[:, :], ALU.mult, ALU.add).then_inc(x_ready, 1)

            def make_shift():
                dve.wait_ge(shift_made, 1)
                dve.wait_ge(gsbs_in, 32)
                V.tensor_copy(shift[:, :], pZ[:, 0:PROJ]).then_inc(shift_ready, 1)

            def fold_link():
                dve.wait_ge(fold_in, 80)
                V.tensor_tensor(gg[:, :], gpq_sb[:, 0, :], gpq_sb[:, 1, :], ALU.mult).then_inc(gg_ready, 1)
                V.scalar_tensor_tensor(fold_sb[:, :, XROWS - 1], bpq_sb[:, 0, :], float(E), bpq_sb[:, 1, :],
                                       ALU.mult, ALU.mult).then_inc(fold_ready, 1)

            def scale_link():
                dve.wait_ge(wx_made, 1)
                V.tensor_scalar(wx[:, :], pW[0:XROWS, :], xscale_sb[:, :], None, ALU.mult).then_inc(pW_free, 1)

            def invert1(q, u):
                n = UNITS * q + u
                w = 2 * (CHUNKS[u][1] - CHUNKS[u][0])
                dve.wait_ge(std1_ready, n + 1)
                after(dve, yn_ready, n - 1)
                V.reciprocal(rstd1[:, u % 2, 0:w], std1[:, u % 2, 0:w]).then_inc(rstd1_ready, 1)

            def norm1(q, u):
                n = UNITS * q + u
                lo, hi = 2 * CHUNKS[u][0], 2 * CHUNKS[u][1]
                w = hi - lo
                dve.wait_ge(rstd1_ready, n + 1)
                after(dve, mixed, n - UNITS + 2)
                V.tensor_tensor(yn[:, lo:hi, :], pY[u % 2][:, 0:w * E].rearrange("p (t e) -> p t e", e=E),
                                rstd1[:, u % 2, 0:w, None].broadcast_to([P, w, E]), ALU.mult).then_inc(yn_ready, 1)

            def affine2(q, u):
                n = UNITS * q + u
                dve.wait_ge(mixed, n + 1)
                after(dve, squared2, n - 1)
                after(dve, t_ready, n - 1)
                V.scalar_tensor_tensor(y2[:, u % 2], pA[u % 2][:, :].rearrange("e (b c) -> e b c", c=PROJ),
                                       gs_sb[:, :], shift[:, None, :].broadcast_to([E, UB, PROJ]),
                                       ALU.mult, ALU.add).then_inc(y2_ready, 1)

            def sum2(q, u):
                n = UNITS * q + u
                dve.wait_ge(squared2, n + 1)
                after(dve, std2_ready, n - 1)
                V.tensor_reduce(ss2[:, u % 2], sq2[:, u % 2], AX.X, ALU.add).then_inc(summed2, 1)

            def invert2(q, u):
                n = UNITS * q + u
                dve.wait_ge(std2_ready, n + 1)
                after(dve, t_ready, n - 1)
                V.reciprocal(rstd2[:, u % 2], std2[:, u % 2]).then_inc(rstd2_ready, 1)

            def place_x(q, u):
                n = UNITS * q + u
                after(dve, cross_done, n - 1)
                g = UG * u
                V.tensor_copy(tx[:, u % 2, :, PROJ:PROJ + 1].rearrange("e (g b) o -> e g (b o)", b=BLOCK),
                              xT[:, q, :, g:g + UG].rearrange("e b g -> e g b")
                              if isinstance(q, int) else
                              xT[:, bass.ds(q, 1), :, g:g + UG].rearrange("e o b g -> e (o g) b")
                              ).then_inc(x_placed, 1)

            def norm2(q, u):
                n = UNITS * q + u
                dve.wait_ge(rstd2_ready, n + 1)
                V.tensor_tensor(tx[:, u % 2, :, 0:PROJ], y2[:, u % 2],
                                rstd2[:, u % 2, :, None].broadcast_to([E, UB, PROJ]), ALU.mult).then_inc(t_ready, 1)

            def relay_on_dve(q, part, samples):
                dve.wait_ge(cross_copied, UNITS * q + UNITS // RELAY * (part + 1))
                relay(V.tensor_copy, part, samples).then_inc(relaid[part], 1)

            def overlay(q):
                if isinstance(q, int) and q == 0:
                    dve.wait_ge(upper_in, 16)
                for part in range(RELAY):
                    dve.wait_ge(relaid_act[part], calls(ACT_RELAYS, part) * (q + 1))
                dve.wait_ge(relaid[RELAY - 1], calls(DVE_RELAYS, RELAY - 1) * (q + 1))
                V.tensor_copy(extraT[2 * PROJ:2 * PROJ + 1, :],
                              sx[0:1, QB * q:QB * (q + 1)] if isinstance(q, int) else
                              sx[0:1, bass.ts(q, QB)]).then_inc(extra_ready, 1)
                V.copy_predicated(pairsT[:, 0:PAIR_TILES, :],
                                  upper_sb[:, :, None].broadcast_to([P, PAIR_TILES, QB]),
                                  pairsT[:, PAIR_TILES:COLUMN_TILES, :]).then_inc(overlaid, 1)

            def link_norm(q):
                dve.wait_ge(linked, q + 1)
                V.bn_stats(wstat[:, :], pL[:, :]).then_inc(link_stats, 1)
                dve.wait_ge(consts_ready, 1)
                dve.wait_ge(link_stats, q + 1)
                V.bn_aggr(wmv[:, :], wstat[:, :]).then_inc(link_mean, 1)
                dve.wait_ge(link_std, q + 1)
                V.reciprocal(wrstd[:, :], wstd[:, :]).then_inc(link_rstd, 1)
                dve.wait_ge(link_rstd, q + 1)
                V.tensor_scalar(zn[:, :], pL[:, 0:DIMS_IN_USE], wmv[:, 0:1], wrstd[:, :],
                                ALU.subtract, ALU.mult).then_inc(z_ready, 1)

            def copy_y(q):
                dve.wait_ge(top3_done, q + 1)
                y_q = y_all[:, q, :] if isinstance(q, int) else y_all[:, bass.ds(q, 1), :].rearrange("o q b -> o (q b)")
                V.tensor_scalar(y_q, pW[0:1, 0:QB], 1.0, None, ALU.mult).then_inc(pW_free, 1)

            def step(i, s):
                first = isinstance(i, int) and i == 0
                if first and s == 0:
                    stats_x()
                    make_shift()
                if first and s == 1:
                    norm_x()
                if first and s == 5:
                    scale_link()
                if (at := unit(i, s, LAG_YN)):
                    invert1(*at)
                if (at := unit(i, s, LAG_Y2)):
                    affine2(*at)
                if (at := quarter(i, s, OVERLAY)):
                    overlay(*at)
                if (at := unit(i, s, LAG_T)):
                    invert2(*at)
                if (at := unit(i, s, LAG_YN)):
                    norm1(*at)
                if first and s == 1:
                    fold_link()
                if first and s == 2:
                    affine_x()
                if (at := unit(i, s, LAG_T)):
                    place_x(*at)
                    norm2(*at)
                if (at := unit(i, s, LAG_Y2)):
                    sum2(*at)
                if first and s < len(MIX) - 1:
                    spread_mix(s + 1)
                for when, part, samples in DVE_RELAYS:
                    if (at := quarter(i, s, when)):
                        relay_on_dve(*at, part, samples)
                if (at := quarter(i, s, LINKED)):
                    link_norm(*at)
                if (at := quarter(i, s, TOP3)):
                    copy_y(*at)

            prepare()
            centre_wsi()
            spread_mix(0)
            run_rounds(dve, step)
            for when, part, samples in DVE_RELAYS:
                if when >= (1, LAG_Z):
                    relay_on_dve(LAST, part, samples)
            overlay(LAST)
            link_norm(LAST)
            dve.wait_ge(z_transposed, LAST + 1)
            for k in range(HZ_ON_ACT, KZ):
                V.tensor_scalar(hz[:, k, :], hz_bank(LAST, k)[:, QB * k:QB * (k + 1)], gl_sb[:, k:k + 1],
                                bl_sb[:, k:k + 1], ALU.mult, ALU.add).then_inc(hz_by_dve, 1)
            for c in range(1, K1, 2):
                dve.wait_ge(top1_done, LAST + c + 1)
                V.tensor_scalar(h1[:, c, :], TOP1_BANKS[c][:, 0:QB], b1_sb[:, c:c + 1], 0.0,
                                ALU.add, ALU.max).then_inc(h1_by_dve, 1)
            copy_y(LAST - 1)
            for c in range(1, K2, 2):
                dve.wait_ge(top2_done, LAST + c + 1)
                V.tensor_scalar(h2[:, c, :], TOP2_BANKS[c][:, 0:QB], b2_sb[:, c:c + 1], 0.0,
                                ALU.add, ALU.max).then_inc(h2_by_dve, 1)
            copy_y(LAST)


def kernel(**inputs):
    import concourse.bacc as bacc
    from concourse.bass_utils import run_bass_kernel_spmd

    a = {name: np.asarray(value) for name, value in inputs.items()}
    tables = [a[f"tbl_{n}"] for n in range(N_SPARSE)]
    f32 = a["W_top1"].dtype

    starts = np.cumsum([0] + [t.shape[0] for t in tables[:-1]]).astype(np.int32)
    bases = np.tile(starts, BATCH).reshape(QUARTERS * TILES, P).T
    ids = a["ids"].reshape(QUARTERS * TILES, P).T

    ws = np.zeros((P, 2, E), f32)
    ws[:D_SPARSE, 0] = ws[D_SPARSE:, 1] = a["L0_rec_Ws"].T

    wsi = a["L0_rec_Wsi"].T[np.arange(PERIOD * P) % N_SPARSE].reshape(PERIOD, P, PROJ).transpose(1, 0, 2)
    owner = np.zeros((P, MIX_COLS // PROJ), f32)
    for u, segs in enumerate(MIX):
        for t, first, count, col in segs:
            for b in range(count):
                sample = (t * P + np.arange(P)) // N_SPARSE
                owner[:, col // PROJ + b] = sample == UB * u + first + b

    dense = a["r_dense_t"].reshape(QUARTERS, GROUPS, BLOCK, KD, P).transpose(4, 3, 0, 2, 1).reshape(P, KD, BATCH)
    wd = a["L0_rec_Wd"].T.reshape(KD, P, E).transpose(1, 0, 2)

    wl = np.zeros((PAIR_TILES * P, MAXD), f32)
    gpq = np.zeros((2, PAIR_TILES * P), f32)
    bpq = np.zeros((2, PAIR_TILES * P), f32)
    fold = np.zeros((PAIR_TILES * P, XROWS), f32)
    g, b = a["L0_rec_gsi"], a["L0_rec_bsi"]
    for r, (p, q, upper) in enumerate(pair_rows()):
        if not (upper and p == q - PROJ // 2):
            hi, lo = max(p, q), min(p, q)
            wl[r] = a["L0_rec_Wl"][:, (hi + 1) * hi // 2 + lo + 1]
            gpq[:, r] = g[p], g[q]
            bpq[:, r] = b[p], b[q]
            fold[r, PROJ + p], fold[r, PROJ + q] = b[q], b[p]
    upper = np.array([u for _, _, u in pair_rows()], np.int32).reshape(PAIR_TILES, P).T
    wlx = a["L0_rec_Wl"][:, [(p + 1) * p // 2 for p in range(PROJ)]].T
    foldx = np.zeros((PROJ, XROWS), f32)
    foldx[np.arange(PROJ), np.arange(PROJ)] = 1
    foldx[:, 2 * PROJ] = b
    xscale = np.concatenate([g, g, np.ones(2, f32)])[:, None]

    def k_tiles(w):
        return w.reshape(-1, P, *w.shape[1:]).swapaxes(0, 1)

    arrays = {
        "tables": np.concatenate(tables), "ids": ids, "bases": bases, "eye": np.eye(P, dtype=f32), "ws": ws,
        "wsi": wsi, "owner": owner, "gs": a["L0_rec_gs"][:, None], "bs": a["L0_rec_bs"][None, :],
        "dense": dense, "wd": wd,
        "gd": a["L0_rec_gd"][:, None], "bd": a["L0_rec_bd"][:, None], "wl": k_tiles(wl), "wlx": wlx, "upper": upper,
        "gpq": gpq.reshape(2, PAIR_TILES, P).transpose(2, 0, 1),
        "bpq": bpq.reshape(2, PAIR_TILES, P).transpose(2, 0, 1),
        "fold": k_tiles(fold), "foldx": foldx, "xscale": xscale,
        "w1": k_tiles(np.concatenate([a["W_top1"][:DIMS_IN_USE], a["W_top1"][MAXD:]])),
        "b1": k_tiles(a["b_top1"]), "w2": k_tiles(a["W_top2"]), "b2": k_tiles(a["b_top2"]),
        "w3": k_tiles(a["W_top3"])[:, :, 0],
        "gl": k_tiles(a["L0_rec_gl"][:DIMS_IN_USE]), "bl": k_tiles(a["L0_rec_bl"][:DIMS_IN_USE]),
    }
    arrays = {f"in_{k}": np.ascontiguousarray(v) for k, v in arrays.items()}

    nc = bacc.Bacc("TRN2", target_bir_lowering=False, num_devices=1)
    args = [nc.dram_tensor(k, v.shape, mybir.dt.from_np(v.dtype), kind="ExternalInput").ap() for k, v in arrays.items()]
    out = nc.dram_tensor("out_y", (1, QUARTERS, QB), mybir.dt.float32, kind="ExternalOutput").ap()
    tower(nc, *args, out)
    r = run_bass_kernel_spmd(nc, [arrays], core_ids=[0])
    y = np.asarray(r.results[0]["out_y"])
    return y.reshape(QUARTERS, BLOCK, GROUPS).transpose(0, 2, 1).reshape(BATCH, 1)
```
